# Optimizing a Trainium2 kernel written in Bass

```python
import numpy as np
import jax
import jax.numpy as jnp

def _softmax(x, axis=-1):
    return jax.nn.softmax(x, axis=axis)

def _gelu(x):
    return jax.nn.gelu(x, approximate=True)

def _silu(x):
    return jax.nn.silu(x)

def _sigmoid(x):
    return jax.nn.sigmoid(x)

def _layernorm(x, axis=-1, eps=1e-05):
    m = jnp.mean(x, axis=axis, keepdims=True)
    v = jnp.var(x, axis=axis, keepdims=True)
    return (x - m) / jnp.sqrt(v + eps)

def _scatter_add(tgt, idx, src, axis=0):
    return tgt.at[idx].add(src)

def _segment_sum(src, seg, n):
    return jax.ops.segment_sum(src, seg, n)
kernel_name = 'mk_flamingo_gated_d4_seqx_r4_817123'

def setup_inputs(seed: int=0):
    np.random.seed(seed)
    _w = jnp.asarray

    def _rec_inputs():
        import jax
        import jax.numpy as jnp
        _rk = jax.random.key(seed)
        x = -0.0002928 + 1 * jax.random.normal(jax.random.fold_in(_rk, 1), (2, 1024, 256), jnp.float32)
        _lenS = 1024 - jax.random.randint(jax.random.fold_in(_rk, 7), (2,), 0, max(1, 1024 // 4) + 1, jnp.int32)
        _lenS2 = 64 - jax.random.randint(jax.random.fold_in(_rk, 8), (2,), 0, max(1, 64 // 4) + 1, jnp.int32)
        _ctx_1024P = jax.random.normal(jax.random.fold_in(_rk, 11), (2, 16, 256), jnp.float32)
        _ctx_1024c = jax.random.dirichlet(jax.random.fold_in(_rk, 511), 0.3 * jnp.ones((16,), jnp.float32), (2, 64))
        _ctx_1024t = jnp.einsum('bsk,bkd->bsd', _ctx_1024c, _ctx_1024P)
        _ctx_1024t = _ctx_1024t * jax.lax.rsqrt(jnp.mean(jnp.square(_ctx_1024t)) + 1e-12) * 0.953939
        ctx_1024 = -1.39393e-06 + 0.999914 * (_ctx_1024t + 0.3 * jax.random.normal(jax.random.fold_in(_rk, 611), (2, 64, 256), jnp.float32))
        fside_Bx16xSxS2_0 = -6.00028e-06 + 0.100001 * jax.random.normal(jax.random.fold_in(_rk, 12), (2, 16, 1024, 64), jnp.float32)
        _validS = jnp.arange(1024)[None, :] < _lenS[:, None]
        _validS2 = jnp.arange(64)[None, :] < _lenS2[:, None]
        _causal = jnp.tril(jnp.ones((1024, 1024), dtype=bool))
        mask_BxSxS2_bf0 = jnp.logical_not(jnp.ones((2, 1024, 64), dtype=bool))
        _g = jax.random.normal(jax.random.fold_in(_rk, 9001), (2, 4), jnp.float32)
        _g = jnp.sign(_g) * jnp.maximum(jnp.abs(_g), 1.0) + (_g == 0) * 1.0
        g_xattn = _g[0]
        g_ffn = _g[1]
        return (x, ctx_1024, fside_Bx16xSxS2_0, mask_BxSxS2_bf0, g_xattn, g_ffn)
    x, ctx_1024, fside_Bx16xSxS2_0, mask_BxSxS2_bf0, g_xattn, g_ffn = _rec_inputs()

    def _L0_xattn_setup():
        import jax, jax.numpy as jnp
        import numpy as np
        import math
        H = 16
        D = 256
        FF = 1024
        DK = D // H
        EPS = 1e-05

        def layer_norm(x, g, b):
            mu = jnp.mean(x, axis=-1, keepdims=True)
            var = jnp.var(x, axis=-1, keepdims=True)
            return (x - mu) * jax.lax.rsqrt(var + EPS) * g + b
        key = jax.random.key(seed)
        ks = jax.random.split(key, 16)
        B, S = (2, 512)
        s = 1.0 / math.sqrt(D)
        return {'x_q': jax.random.normal(ks[0], (B, S, D), jnp.float32), 'x_kv': jax.random.normal(ks[1], (B, S, D), jnp.float32), 'bias': jax.random.normal(ks[2], (B, H, S, S), jnp.float32) * 0.1, 'Wq': jax.random.normal(ks[3], (D, D), jnp.float32) * s, 'Wk': jax.random.normal(ks[4], (D, D), jnp.float32) * s, 'Wv': jax.random.normal(ks[5], (D, D), jnp.float32) * s, 'Wo': jax.random.normal(ks[6], (D, D), jnp.float32) * s, 'W1': jax.random.normal(ks[7], (FF, D), jnp.float32) * s, 'b1': jnp.zeros((FF,), jnp.float32), 'W2': jax.random.normal(ks[8], (D, FF), jnp.float32) * (1.0 / math.sqrt(FF)), 'b2': jnp.zeros((D,), jnp.float32), 'g1': jnp.ones((D,), jnp.float32), 'be1': jnp.zeros((D,), jnp.float32), 'g2': jnp.ones((D,), jnp.float32), 'be2': jnp.zeros((D,), jnp.float32)}
    _L0_xattn_all = _L0_xattn_setup()
    _L0_xattn_in = {k: v for k, v in _L0_xattn_all.items() if k in ('Wq', 'Wk', 'Wv', 'Wo', 'W1', 'b1', 'W2', 'b2', 'g1', 'be1', 'g2', 'be2')}
    del _L0_xattn_all

    def _L0_ffn_setup():
        import jax, jax.numpy as jnp
        import numpy as np
        IN_F = 256
        OUT_F = 256
        N_EXPERTS = 8
        TOP_K = 2
        key = jax.random.key(seed)
        ks = jax.random.split(key, 5)
        scale_in = 1.0 / np.sqrt(IN_F)
        x = jax.random.normal(ks[0], (4, 512, IN_F), dtype=jnp.float32)
        W_experts = jax.random.uniform(ks[1], (N_EXPERTS, OUT_F, IN_F), jnp.float32, -scale_in, scale_in)
        b_experts = jax.random.uniform(ks[2], (N_EXPERTS, OUT_F), jnp.float32, -scale_in, scale_in)
        W_router = jax.random.uniform(ks[3], (N_EXPERTS, IN_F), jnp.float32, -scale_in, scale_in)
        b_router = jax.random.uniform(ks[4], (N_EXPERTS,), jnp.float32, -scale_in, scale_in)
        return {'x': x, 'W_experts': W_experts, 'b_experts': b_experts, 'W_router': W_router, 'b_router': b_router}
    _L0_ffn_all = _L0_ffn_setup()
    _L0_ffn_in = {k: v for k, v in _L0_ffn_all.items() if k in ('W_experts', 'b_experts', 'W_router', 'b_router')}
    del _L0_ffn_all

    def _L1_xattn_setup():
        import jax, jax.numpy as jnp
        import numpy as np
        D_MODEL = 256
        NUM_HEADS = 16
        D_K = D_MODEL // NUM_HEADS

        def _split_heads(x):
            B, S, D = x.shape
            return x.reshape(B, S, NUM_HEADS, D_K).transpose(0, 2, 1, 3)
        key = jax.random.key(seed)
        ks = jax.random.split(key, 11)
        B, S, D = (2, 512, D_MODEL)
        s = 1.0 / np.sqrt(D)
        return {'Q': jax.random.normal(ks[0], (B, S, D), jnp.float32), 'K': jax.random.normal(ks[1], (B, S, D), jnp.float32), 'V': jax.random.normal(ks[2], (B, S, D), jnp.float32), 'Wq': jax.random.normal(ks[3], (D, D), jnp.float32) * s, 'bq': jax.random.normal(ks[4], (D,), jnp.float32) * s, 'Wk': jax.random.normal(ks[5], (D, D), jnp.float32) * s, 'bk': jax.random.normal(ks[6], (D,), jnp.float32) * s, 'Wv': jax.random.normal(ks[7], (D, D), jnp.float32) * s, 'bv': jax.random.normal(ks[8], (D,), jnp.float32) * s, 'Wo': jax.random.normal(ks[9], (D, D), jnp.float32) * s, 'bo': jax.random.normal(ks[10], (D,), jnp.float32) * s}
    _L1_xattn_all = _L1_xattn_setup()
    _L1_xattn_in = {k: v for k, v in _L1_xattn_all.items() if k in ('Wq', 'bq', 'Wk', 'bk', 'Wv', 'bv', 'Wo', 'bo')}
    del _L1_xattn_all

    def _L1_ffn_setup():
        import jax, jax.numpy as jnp
        import numpy as np
        TOP_K = 2
        NUM_EXPERTS = 8
        HIDDEN = 256
        INTER = 512
        key = jax.random.key(seed)
        ks = jax.random.split(key, 5)
        s_h = 1.0 / np.sqrt(HIDDEN)
        s_i = 1.0 / np.sqrt(INTER)
        return {'hidden_states': jax.random.normal(ks[0], (4, 1024, HIDDEN), dtype=jnp.float32), 'router_w': jax.random.uniform(ks[1], (NUM_EXPERTS, HIDDEN), minval=-s_h, maxval=s_h, dtype=jnp.float32), 'gate_w': jax.random.uniform(ks[2], (NUM_EXPERTS, HIDDEN, INTER), minval=-s_h, maxval=s_h, dtype=jnp.float32), 'up_w': jax.random.uniform(ks[3], (NUM_EXPERTS, HIDDEN, INTER), minval=-s_h, maxval=s_h, dtype=jnp.float32), 'down_w': jax.random.uniform(ks[4], (NUM_EXPERTS, INTER, HIDDEN), minval=-s_i, maxval=s_i, dtype=jnp.float32)}
    _L1_ffn_all = _L1_ffn_setup()
    _L1_ffn_in = {k: v for k, v in _L1_ffn_all.items() if k in ('router_w', 'gate_w', 'up_w', 'down_w')}
    del _L1_ffn_all

    def _L2_xattn_setup():
        import jax, jax.numpy as jnp
        import numpy as np
        D_MODEL = 256
        NUM_HEADS = 16
        HEAD_DIM = D_MODEL // NUM_HEADS
        key = jax.random.key(seed)
        ks = jax.random.split(key, 11)
        B, S = (2, 512)
        scale = 1.0 / np.sqrt(D_MODEL)
        inp = {'query': jax.random.normal(ks[0], (B, S, D_MODEL), jnp.float32), 'key': jax.random.normal(ks[1], (B, S, D_MODEL), jnp.float32), 'value': jax.random.normal(ks[2], (B, S, D_MODEL), jnp.float32), 'Wq': jax.random.normal(ks[3], (D_MODEL, D_MODEL), jnp.float32) * scale, 'bq': jnp.zeros((D_MODEL,), jnp.float32), 'Wk': jax.random.normal(ks[4], (D_MODEL, D_MODEL), jnp.float32) * scale, 'bk': jnp.zeros((D_MODEL,), jnp.float32), 'Wv': jax.random.normal(ks[5], (D_MODEL, D_MODEL), jnp.float32) * scale, 'bv': jnp.zeros((D_MODEL,), jnp.float32), 'Wo': jax.random.normal(ks[6], (D_MODEL, D_MODEL), jnp.float32) * scale, 'bo': jnp.zeros((D_MODEL,), jnp.float32)}
        return inp
    _L2_xattn_all = _L2_xattn_setup()
    _L2_xattn_in = {k: v for k, v in _L2_xattn_all.items() if k in ('Wq', 'bq', 'Wk', 'bk', 'Wv', 'bv', 'Wo', 'bo')}
    del _L2_xattn_all

    def _L2_ffn_setup():
        import jax, jax.numpy as jnp
        import numpy as np
        BLOCK = 16
        _GRID = jnp.array([0.0, 0.5, 1.0, 1.5, 2.0, 3.0, 4.0, 6.0], dtype=jnp.float32)
        _MID = jnp.array([0.25, 0.75, 1.25, 1.75, 2.5, 3.5, 5.0], dtype=jnp.float32)

        def fp4_quant_dequant(x):
            shape = x.shape
            xb = x.reshape(shape[:-1] + (shape[-1] // BLOCK, BLOCK))
            scale = jnp.max(jnp.abs(xb), axis=-1, keepdims=True) / 6.0
            scale = jnp.maximum(scale, jnp.float32(1e-12))
            xn = xb / scale
            idx = jnp.searchsorted(_MID, jnp.abs(xn))
            q = _GRID[idx] * jnp.sign(xn) * scale
            return q.reshape(shape)

        def fp4_linear(x, w):
            xq = fp4_quant_dequant(x)
            wq = fp4_quant_dequant(w)
            return jnp.einsum('bsk,nk->bsn', xq, wq)
        key = jax.random.key(seed)
        k1, k2, k3, k4 = jax.random.split(key, 4)
        H, I = (256, 704)
        x = jax.random.normal(k1, (4, 1024, H), dtype=jnp.float32)
        w_gate = jax.random.normal(k2, (I, H), dtype=jnp.float32) * 0.02
        w_up = jax.random.normal(k3, (I, H), dtype=jnp.float32) * 0.02
        w_down = jax.random.normal(k4, (H, I), dtype=jnp.float32) * 0.02
        return {'x': x, 'w_gate': w_gate, 'w_up': w_up, 'w_down': w_down}
    _L2_ffn_all = _L2_ffn_setup()
    _L2_ffn_in = {k: v for k, v in _L2_ffn_all.items() if k in ('w_gate', 'w_up', 'w_down')}
    del _L2_ffn_all

    def _L3_xattn_setup():
        import jax, jax.numpy as jnp
        import numpy as np
        HIDDEN = 256
        HEADS = 16
        D_K = HIDDEN // HEADS
        B, LQ, LKV = (4, 256, 512)
        NEG_INF = -1e+18
        key = jax.random.key(seed)
        ks = jax.random.split(key, 12)
        s = 1.0 / np.sqrt(HIDDEN)
        return {'tgt': jax.random.normal(ks[0], (B, LQ, HIDDEN), jnp.float32), 'memory': jax.random.normal(ks[1], (B, LKV, HIDDEN), jnp.float32), 'mask': jnp.zeros((B, LQ, LKV), dtype=bool), 'Wq': jax.random.normal(ks[2], (HIDDEN, HIDDEN), jnp.float32) * s, 'bq': jnp.zeros((HIDDEN,), jnp.float32), 'Wk': jax.random.normal(ks[3], (HIDDEN, HIDDEN), jnp.float32) * s, 'bk': jnp.zeros((HIDDEN,), jnp.float32), 'Wv': jax.random.normal(ks[4], (HIDDEN, HIDDEN), jnp.float32) * s, 'bv': jnp.zeros((HIDDEN,), jnp.float32), 'Wo': jax.random.normal(ks[5], (HIDDEN, HIDDEN), jnp.float32) * s, 'bo': jnp.zeros((HIDDEN,), jnp.float32)}
    _L3_xattn_all = _L3_xattn_setup()
    _L3_xattn_in = {k: v for k, v in _L3_xattn_all.items() if k in ('Wq', 'bq', 'Wk', 'bk', 'Wv', 'bv', 'Wo', 'bo')}
    del _L3_xattn_all

    def _L3_ffn_setup():
        import jax, jax.numpy as jnp
        import numpy as np
        D, H, O, E, TOPK = (256, 1024, 256, 8, 2)
        B, S = (4, 256)
        key = jax.random.key(seed)
        ks = jax.random.split(key, 12)
        std = 0.02
        return {'hidden_states': jax.random.normal(ks[0], (B, S, D), dtype=jnp.float32), 'norm_weight': jnp.ones((D,), dtype=jnp.float32), 'router_w': jax.random.normal(ks[1], (E, D), dtype=jnp.float32) * std, 'sw1': jax.random.normal(ks[2], (D, H), dtype=jnp.float32) * (1.0 / np.sqrt(D)), 'sb1': jnp.zeros((H,), dtype=jnp.float32), 'sw2': jax.random.normal(ks[3], (H, O), dtype=jnp.float32) * (1.0 / np.sqrt(H)), 'sb2': jnp.zeros((O,), dtype=jnp.float32), 'ew1': jax.random.normal(ks[4], (E, D, H), dtype=jnp.float32) * (1.0 / np.sqrt(D)), 'eb1': jnp.zeros((E, H), dtype=jnp.float32), 'ew2': jax.random.normal(ks[5], (E, H, O), dtype=jnp.float32) * (1.0 / np.sqrt(H)), 'eb2': jnp.zeros((E, O), dtype=jnp.float32)}
    _L3_ffn_all = _L3_ffn_setup()
    _L3_ffn_in = {k: v for k, v in _L3_ffn_all.items() if k in ('norm_weight', 'router_w', 'sw1', 'sb1', 'sw2', 'sb2', 'ew1', 'eb1', 'ew2', 'eb2')}
    del _L3_ffn_all
    return {'x': x, 'ctx_1024': ctx_1024, 'fside_Bx16xSxS2_0': fside_Bx16xSxS2_0, 'mask_BxSxS2_bf0': mask_BxSxS2_bf0, 'g_xattn': g_xattn, 'g_ffn': g_ffn, 'L0_xattn_Wq': _L0_xattn_in['Wq'], 'L0_xattn_Wk': _L0_xattn_in['Wk'], 'L0_xattn_Wv': _L0_xattn_in['Wv'], 'L0_xattn_Wo': _L0_xattn_in['Wo'], 'L0_xattn_W1': _L0_xattn_in['W1'], 'L0_xattn_b1': _L0_xattn_in['b1'], 'L0_xattn_W2': _L0_xattn_in['W2'], 'L0_xattn_b2': _L0_xattn_in['b2'], 'L0_xattn_g1': _L0_xattn_in['g1'], 'L0_xattn_be1': _L0_xattn_in['be1'], 'L0_xattn_g2': _L0_xattn_in['g2'], 'L0_xattn_be2': _L0_xattn_in['be2'], 'L0_ffn_W_experts': _L0_ffn_in['W_experts'], 'L0_ffn_b_experts': _L0_ffn_in['b_experts'], 'L0_ffn_W_router': _L0_ffn_in['W_router'], 'L0_ffn_b_router': _L0_ffn_in['b_router'], 'L1_xattn_Wq': _L1_xattn_in['Wq'], 'L1_xattn_bq': _L1_xattn_in['bq'], 'L1_xattn_Wk': _L1_xattn_in['Wk'], 'L1_xattn_bk': _L1_xattn_in['bk'], 'L1_xattn_Wv': _L1_xattn_in['Wv'], 'L1_xattn_bv': _L1_xattn_in['bv'], 'L1_xattn_Wo': _L1_xattn_in['Wo'], 'L1_xattn_bo': _L1_xattn_in['bo'], 'L1_ffn_router_w': _L1_ffn_in['router_w'], 'L1_ffn_gate_w': _L1_ffn_in['gate_w'], 'L1_ffn_up_w': _L1_ffn_in['up_w'], 'L1_ffn_down_w': _L1_ffn_in['down_w'], 'L2_xattn_Wq': _L2_xattn_in['Wq'], 'L2_xattn_bq': _L2_xattn_in['bq'], 'L2_xattn_Wk': _L2_xattn_in['Wk'], 'L2_xattn_bk': _L2_xattn_in['bk'], 'L2_xattn_Wv': _L2_xattn_in['Wv'], 'L2_xattn_bv': _L2_xattn_in['bv'], 'L2_xattn_Wo': _L2_xattn_in['Wo'], 'L2_xattn_bo': _L2_xattn_in['bo'], 'L2_ffn_w_gate': _L2_ffn_in['w_gate'], 'L2_ffn_w_up': _L2_ffn_in['w_up'], 'L2_ffn_w_down': _L2_ffn_in['w_down'], 'L3_xattn_Wq': _L3_xattn_in['Wq'], 'L3_xattn_bq': _L3_xattn_in['bq'], 'L3_xattn_Wk': _L3_xattn_in['Wk'], 'L3_xattn_bk': _L3_xattn_in['bk'], 'L3_xattn_Wv': _L3_xattn_in['Wv'], 'L3_xattn_bv': _L3_xattn_in['bv'], 'L3_xattn_Wo': _L3_xattn_in['Wo'], 'L3_xattn_bo': _L3_xattn_in['bo'], 'L3_ffn_norm_weight': _L3_ffn_in['norm_weight'], 'L3_ffn_router_w': _L3_ffn_in['router_w'], 'L3_ffn_sw1': _L3_ffn_in['sw1'], 'L3_ffn_sb1': _L3_ffn_in['sb1'], 'L3_ffn_sw2': _L3_ffn_in['sw2'], 'L3_ffn_sb2': _L3_ffn_in['sb2'], 'L3_ffn_ew1': _L3_ffn_in['ew1'], 'L3_ffn_eb1': _L3_ffn_in['eb1'], 'L3_ffn_ew2': _L3_ffn_in['ew2'], 'L3_ffn_eb2': _L3_ffn_in['eb2']}

def reference(x, ctx_1024, fside_Bx16xSxS2_0, mask_BxSxS2_bf0, g_xattn, g_ffn, L0_xattn_Wq, L0_xattn_Wk, L0_xattn_Wv, L0_xattn_Wo, L0_xattn_W1, L0_xattn_b1, L0_xattn_W2, L0_xattn_b2, L0_xattn_g1, L0_xattn_be1, L0_xattn_g2, L0_xattn_be2, L0_ffn_W_experts, L0_ffn_b_experts, L0_ffn_W_router, L0_ffn_b_router, L1_xattn_Wq, L1_xattn_bq, L1_xattn_Wk, L1_xattn_bk, L1_xattn_Wv, L1_xattn_bv, L1_xattn_Wo, L1_xattn_bo, L1_ffn_router_w, L1_ffn_gate_w, L1_ffn_up_w, L1_ffn_down_w, L2_xattn_Wq, L2_xattn_bq, L2_xattn_Wk, L2_xattn_bk, L2_xattn_Wv, L2_xattn_bv, L2_xattn_Wo, L2_xattn_bo, L2_ffn_w_gate, L2_ffn_w_up, L2_ffn_w_down, L3_xattn_Wq, L3_xattn_bq, L3_xattn_Wk, L3_xattn_bk, L3_xattn_Wv, L3_xattn_bv, L3_xattn_Wo, L3_xattn_bo, L3_ffn_norm_weight, L3_ffn_router_w, L3_ffn_sw1, L3_ffn_sb1, L3_ffn_sw2, L3_ffn_sb2, L3_ffn_ew1, L3_ffn_eb1, L3_ffn_ew2, L3_ffn_eb2):
    import jax
    import jax.numpy as jnp

    def _L0_xattn_ref(x_q, x_kv, bias, Wq, Wk, Wv, Wo, W1, b1, W2, b2, g1, be1, g2, be2):
        import jax, jax.numpy as jnp
        import numpy as np
        import math
        H = 16
        D = 256
        FF = 1024
        DK = D // H
        EPS = 1e-05

        def layer_norm(x, g, b):
            mu = jnp.mean(x, axis=-1, keepdims=True)
            var = jnp.var(x, axis=-1, keepdims=True)
            return (x - mu) * jax.lax.rsqrt(var + EPS) * g + b
        B, S, _ = x_q.shape

        def split(x):
            return x.reshape(B, -1, H, DK).transpose(0, 2, 1, 3)
        q = split(x_q @ Wq.T)
        k = split(x_kv @ Wk.T)
        v = split(x_kv @ Wv.T)
        scores = jnp.einsum('bhqd,bhkd->bhqk', q, k) / math.sqrt(DK) + bias
        p = jax.nn.softmax(scores, axis=-1)
        o = jnp.einsum('bhqk,bhkd->bhqd', p, v)
        o = o.transpose(0, 2, 1, 3).reshape(B, S, D)
        x = x_q + o @ Wo.T
        h = jax.nn.gelu(layer_norm(x, g1, be1) @ W1.T + b1, approximate=False)
        x = x + h @ W2.T + b2
        return layer_norm(x, g2, be2)

    def _L0_ffn_ref(x, W_experts, b_experts, W_router, b_router):
        import jax, jax.numpy as jnp
        import numpy as np
        IN_F = 256
        OUT_F = 256
        N_EXPERTS = 8
        TOP_K = 2
        router_logits = jnp.einsum('bsd,ed->bse', x, W_router) + b_router
        router_weights = jax.nn.softmax(router_logits, axis=-1)
        if TOP_K < N_EXPERTS:
            topk_w, topk_idx = jax.lax.top_k(router_weights, TOP_K)
            sparse = jnp.zeros_like(router_weights)
            router_weights = jnp.take_along_axis(sparse, topk_idx, axis=-1)
            router_weights = sparse.at[..., :].set(0.0)
            b_idx = jnp.arange(sparse.shape[0])[:, None, None]
            s_idx = jnp.arange(sparse.shape[1])[None, :, None]
            router_weights = sparse.at[b_idx, s_idx, topk_idx].set(topk_w)
        expert_out = jnp.einsum('bsd,eod->bseo', x, W_experts) + b_experts
        return jnp.einsum('bseo,bse->bso', expert_out, router_weights)

    def _L1_xattn_ref(Q, K, V, Wq, bq, Wk, bk, Wv, bv, Wo, bo):
        import jax, jax.numpy as jnp
        import numpy as np
        D_MODEL = 256
        NUM_HEADS = 16
        D_K = D_MODEL // NUM_HEADS

        def _split_heads(x):
            B, S, D = x.shape
            return x.reshape(B, S, NUM_HEADS, D_K).transpose(0, 2, 1, 3)
        q = _split_heads(Q @ Wq + bq)
        k = _split_heads(K @ Wk + bk)
        v = _split_heads(V @ Wv + bv)
        scale = 1.0 / np.sqrt(D_K)
        scores = jnp.einsum('bhqd,bhkd->bhqk', q, k) * scale
        P = jax.nn.softmax(scores, axis=-1)
        O = jnp.einsum('bhqk,bhkd->bhqd', P, v)
        B, H, S, dk = O.shape
        O = O.transpose(0, 2, 1, 3).reshape(B, S, H * dk)
        return O @ Wo + bo

    def _L1_ffn_ref(hidden_states, router_w, gate_w, up_w, down_w):
        import jax, jax.numpy as jnp
        import numpy as np
        TOP_K = 2
        NUM_EXPERTS = 8
        HIDDEN = 256
        INTER = 512
        B, S, H = hidden_states.shape
        x = hidden_states.reshape(-1, H)
        T = x.shape[0]
        logits = x @ router_w.T
        probs = jax.nn.softmax(logits.astype(jnp.float32), axis=-1)
        w, sel = jax.lax.top_k(probs, TOP_K)
        w = w / jnp.sum(w, axis=-1, keepdims=True)
        w = w.astype(x.dtype)
        combine = jnp.zeros((T, NUM_EXPERTS), dtype=x.dtype)
        combine = combine.at[jnp.arange(T)[:, None], sel].add(w)

        def body(acc, ew):
            g, u, d, c = ew
            h = jax.nn.silu(x @ g) * (x @ u)
            return (acc + c[:, None] * (h @ d), None)
        acc0 = jnp.zeros((T, H), dtype=x.dtype)
        out, _ = jax.lax.scan(body, acc0, (gate_w, up_w, down_w, combine.T))
        return out.reshape(B, S, H)

    def _L2_xattn_ref(query, key, value, Wq, bq, Wk, bk, Wv, bv, Wo, bo):
        import jax, jax.numpy as jnp
        import numpy as np
        D_MODEL = 256
        NUM_HEADS = 16
        HEAD_DIM = D_MODEL // NUM_HEADS
        B, S, _ = query.shape
        q = query @ Wq + bq
        k = key @ Wk + bk
        v = value @ Wv + bv
        q = q.reshape(B, S, NUM_HEADS, HEAD_DIM).transpose(0, 2, 1, 3)
        k = k.reshape(B, -1, NUM_HEADS, HEAD_DIM).transpose(0, 2, 1, 3)
        v = v.reshape(B, -1, NUM_HEADS, HEAD_DIM).transpose(0, 2, 1, 3)
        scores = jnp.einsum('bhqd,bhkd->bhqk', q, k) / jnp.sqrt(jnp.asarray(HEAD_DIM, q.dtype))
        attn = jax.nn.softmax(scores, axis=-1)
        out = jnp.einsum('bhqk,bhkd->bhqd', attn, v)
        out = out.transpose(0, 2, 1, 3).reshape(B, S, D_MODEL)
        return out @ Wo + bo

    def _L2_ffn_ref(x, w_gate, w_up, w_down):
        import jax, jax.numpy as jnp
        import numpy as np
        BLOCK = 16
        _GRID = jnp.array([0.0, 0.5, 1.0, 1.5, 2.0, 3.0, 4.0, 6.0], dtype=jnp.float32)
        _MID = jnp.array([0.25, 0.75, 1.25, 1.75, 2.5, 3.5, 5.0], dtype=jnp.float32)

        def fp4_quant_dequant(x):
            shape = x.shape
            xb = x.reshape(shape[:-1] + (shape[-1] // BLOCK, BLOCK))
            scale = jnp.max(jnp.abs(xb), axis=-1, keepdims=True) / 6.0
            scale = jnp.maximum(scale, jnp.float32(1e-12))
            xn = xb / scale
            idx = jnp.searchsorted(_MID, jnp.abs(xn))
            q = _GRID[idx] * jnp.sign(xn) * scale
            return q.reshape(shape)

        def fp4_linear(x, w):
            xq = fp4_quant_dequant(x)
            wq = fp4_quant_dequant(w)
            return jnp.einsum('bsk,nk->bsn', xq, wq)
        gate = fp4_linear(x, w_gate)
        y = fp4_linear(x, w_up)
        h = jax.nn.silu(gate) * y
        return fp4_linear(h, w_down)

    def _L3_xattn_ref(tgt, memory, mask, Wq, bq, Wk, bk, Wv, bv, Wo, bo):
        import jax, jax.numpy as jnp
        import numpy as np
        HIDDEN = 256
        HEADS = 16
        D_K = HIDDEN // HEADS
        B, LQ, LKV = (4, 256, 512)
        NEG_INF = -1e+18
        b = tgt.shape[0]

        def heads(x):
            return x.reshape(b, -1, HEADS, D_K).transpose(0, 2, 1, 3)
        q = heads(tgt @ Wq + bq) / jnp.sqrt(jnp.asarray(D_K, tgt.dtype))
        k = heads(memory @ Wk + bk)
        v = heads(memory @ Wv + bv)
        scores = jnp.einsum('bhqd,bhkd->bhqk', q, k)
        scores = jnp.where(mask[:, None, :, :], NEG_INF, scores)
        attn = jax.nn.softmax(scores, axis=-1)
        ctx = jnp.einsum('bhqk,bhkd->bhqd', attn, v)
        ctx = ctx.transpose(0, 2, 1, 3).reshape(b, -1, HIDDEN)
        return ctx @ Wo + bo

    def _L3_ffn_ref(hidden_states, norm_weight, router_w, sw1, sb1, sw2, sb2, ew1, eb1, ew2, eb2):
        import jax, jax.numpy as jnp
        import numpy as np
        D, H, O, E, TOPK = (256, 1024, 256, 8, 2)
        B, S = (4, 256)
        b, s, d = hidden_states.shape
        var = jnp.mean(jnp.square(hidden_states), axis=-1, keepdims=True)
        normed = hidden_states * jax.lax.rsqrt(var + 1e-08) * norm_weight
        shared = jnp.maximum(normed @ sw1 + sb1, 0.0) @ sw2 + sb2
        flat = normed.reshape(-1, d)
        T = flat.shape[0]
        probs = jax.nn.sigmoid(flat @ router_w.T)
        scores, idx = jax.lax.top_k(probs, TOPK)
        w = scores / (jnp.sum(scores, axis=-1, keepdims=True) + 1e-06)
        comb = jnp.zeros((T, E), dtype=flat.dtype)
        comb = comb.at[jnp.arange(T)[:, None], idx].add(w)
        h = jnp.maximum(jnp.einsum('td,edh->teh', flat, ew1) + eb1[None, :, :], 0.0)
        eo = jnp.einsum('teh,eho->teo', h, ew2) + eb2[None, :, :]
        routed = jnp.einsum('teo,te->to', eo, comb)
        return shared + routed.reshape(b, s, -1)
    x = x + jnp.tanh(g_xattn[0]) * _L0_xattn_ref(_layernorm(x, axis=-1), ctx_1024, fside_Bx16xSxS2_0, L0_xattn_Wq, L0_xattn_Wk, L0_xattn_Wv, L0_xattn_Wo, L0_xattn_W1, L0_xattn_b1, L0_xattn_W2, L0_xattn_b2, L0_xattn_g1, L0_xattn_be1, L0_xattn_g2, L0_xattn_be2)
    x = x + jnp.tanh(g_ffn[0]) * _L0_ffn_ref(_layernorm(x, axis=-1), L0_ffn_W_experts, L0_ffn_b_experts, L0_ffn_W_router, L0_ffn_b_router)
    x = x + jnp.tanh(g_xattn[1]) * _L1_xattn_ref(_layernorm(x, axis=-1), ctx_1024, ctx_1024, L1_xattn_Wq, L1_xattn_bq, L1_xattn_Wk, L1_xattn_bk, L1_xattn_Wv, L1_xattn_bv, L1_xattn_Wo, L1_xattn_bo)
    x = x + jnp.tanh(g_ffn[1]) * _L1_ffn_ref(_layernorm(x, axis=-1), L1_ffn_router_w, L1_ffn_gate_w, L1_ffn_up_w, L1_ffn_down_w)
    x = x + jnp.tanh(g_xattn[2]) * _L2_xattn_ref(_layernorm(x, axis=-1), ctx_1024, ctx_1024, L2_xattn_Wq, L2_xattn_bq, L2_xattn_Wk, L2_xattn_bk, L2_xattn_Wv, L2_xattn_bv, L2_xattn_Wo, L2_xattn_bo)
    x = x + jnp.tanh(g_ffn[2]) * _L2_ffn_ref(_layernorm(x, axis=-1), L2_ffn_w_gate, L2_ffn_w_up, L2_ffn_w_down)
    x = x + jnp.tanh(g_xattn[3]) * _L3_xattn_ref(_layernorm(x, axis=-1), ctx_1024, mask_BxSxS2_bf0, L3_xattn_Wq, L3_xattn_bq, L3_xattn_Wk, L3_xattn_bk, L3_xattn_Wv, L3_xattn_bv, L3_xattn_Wo, L3_xattn_bo)
    x = x + jnp.tanh(g_ffn[3]) * _L3_ffn_ref(_layernorm(x, axis=-1), L3_ffn_norm_weight, L3_ffn_router_w, L3_ffn_sw1, L3_ffn_sb1, L3_ffn_sw2, L3_ffn_sb2, L3_ffn_ew1, L3_ffn_eb1, L3_ffn_ew2, L3_ffn_eb2)
    return x

_drawn_inputs = setup_inputs


def setup_inputs(seed=0):
    import zlib

    import numpy as np

    out = dict(_drawn_inputs(seed))
    spreads = {'L0_xattn_b1': (0.0, 0.1),
     'L0_xattn_b2': (0.0, 0.1),
     'L0_xattn_g1': (1.0, 0.2),
     'L0_xattn_be1': (0.0, 0.1),
     'L0_xattn_g2': (1.0, 0.2),
     'L0_xattn_be2': (0.0, 0.1),
     'L2_xattn_bq': (0.0, 0.343),
     'L2_xattn_bk': (0.0, 2.0),
     'L2_xattn_bv': (0.0, 0.1),
     'L2_xattn_bo': (0.0, 0.1),
     'L3_xattn_bq': (0.0, 0.285),
     'L3_xattn_bk': (0.0, 2.0),
     'L3_xattn_bv': (0.0, 0.1),
     'L3_xattn_bo': (0.0, 0.1),
     'L3_ffn_norm_weight': (1.0, 0.2),
     'L3_ffn_sb1': (0.0, 0.1),
     'L3_ffn_sb2': (0.0, 0.1),
     'L3_ffn_eb1': (0.0, 0.379),
     'L3_ffn_eb2': (0.0, 0.1)}
    factors = {'fside_Bx16xSxS2_0': 3.369,
     'g_ffn': 23.264,
     'L0_ffn_b_experts': 3.268,
     'L1_xattn_bk': 64.0}
    for name, (base, spread) in spreads.items():
        noise = np.random.default_rng([zlib.crc32(name.encode()), seed]).standard_normal(out[name].shape)
        drawn = base * np.exp(spread * noise) if base else spread * noise
        out[name] = jnp.asarray(drawn.astype(out[name].dtype))
    for name, factor in factors.items():
        out[name] = (out[name] * factor).astype(out[name].dtype)
    return out
```

```python
from contextlib import ExitStack

import concourse.bass as bass
from concourse import mybir

ALU = mybir.AluOpType
ACT = mybir.ActivationFunctionType
AX = mybir.AxisListType.X
F32 = mybir.dt.float32
F32R = mybir.dt.float32r
BF16 = mybir.dt.bfloat16
U32 = mybir.dt.uint32
U8 = mybir.dt.uint8

P = 128
D = 256
KC = D // P
TOK = 2048
NT = TOK // P
GT = 4
GW = GT * P
NG = NT // GT
NB = 2
S2 = 64
H = 16
DK = D // H
SCALE = DK ** -0.5
HC = P // DK
SC = HC * S2
VC = P + HC
NE = 8
EPS = 1e-5
UH = 512
UC = UH // P
HL = ((0, 0), (0, 1), (1, 0))
ENGINES = 5
FP4_MID = ((0.25, 0.5), (0.75, 0.5), (1.25, 0.5), (1.75, 0.5), (2.5, 1.0), (3.5, 1.0), (5.0, 2.0))
FB = 16
FI = 704
FR = 88
FN = FI // FR
LAYERS = 4
TURNS = {name: n for n, name in enumerate(("at0", "gelu", "experts0", "at1", "swiglu", "at2", "fp4", "at3", "relu"))}


class Steps:

    def __init__(self, eng, sem, base=0):
        self.eng, self.sem, self.base, self.n = eng, sem, base, 0

    def __call__(self, ins, hold=None):
        self.n += 1
        ins.then_inc(self.sem, 1)
        self.eng.wait_ge(self.sem, self.base + self.n)
        if hold is not None:
            self.eng.sem_inc(hold, 1)


def build(nc, A, out, stop=99):
    with ExitStack() as ctx:
        def sb(name, shape, dt=F32):
            return ctx.enter_context(nc.sbuf_tensor(name, shape, dt))

        def sem(name):
            return ctx.enter_context(nc.semaphore(name))

        X = sb("X", [P, NT, D])
        Y = sb("Y", [P, NT, D])
        RA = sb("RA", [P, 28672], F32R)
        FA = sb("FA", [P, 9216])
        ident = sb("ident", [P, P])
        iota8 = sb("iota8", [P, NE])
        headmask = sb("headmask", [P, HC])
        gates = sb("gates", [P, 2 * LAYERS])
        neghalf = sb("neghalf", [P, GT])
        negbig = sb("negbig", [P, 1])
        mask = sb("mask", [P, NT, S2], U8)
        mask_g = sb("mask_g", [P, GT, S2], U8)
        unit_bias = sb("unit_bias", [P, 2, UC])
        KT = sb("KT", [P, LAYERS, KC, P])
        VD = sb("VD", [P, LAYERS, NB, D])
        VBF = sb("VBF", [P, NB * H // 2 * VC + 5 * 2 * DK])
        VB = VBF[:, 0:NB * H // 2 * VC].rearrange("p (b c v) -> p b c v", b=NB, c=H // 2)
        bias_cols = sb("bias_cols", [P, 2 * LAYERS * KC + 8 + 72])
        coef = sb("coef", [P, NT, 18])
        stats = sb("stats", [P, GT, 6])
        meanvar = sb("meanvar", [P, GT, 2])
        vareps = sb("vareps", [P, GT])
        rstd = sb("rstd", [P, GT])
        rms = sb("rms", [P, GT])
        small = sb("small", [P, 64])
        router_r = sb("router_r", [P, 2, KC, P], F32R)
        PS = ctx.enter_context(nc.psum_tensor("PS", [P, 8, 512], F32))

        sems = {}

        def shared(name):
            if name not in sems:
                sems[name] = sem(name)
            return sems[name]

        def rview(off, *dims):
            return _view(RA, off, dims)

        def fview(off, *dims):
            return _view(FA, off, dims)

        bar = sem("phase_done")
        held = sem("held")
        phases = []
        steps_done = []

        bq_col = lambda l: (2 * l) * KC
        bk_col = lambda l: (2 * l + 1) * KC
        B1_COL = 2 * LAYERS * KC
        EB_COL = B1_COL + 8

        class Norm:

            def __init__(self, turn, src, xn, xt_hi, xt_lo, affine=None, rms_row=None, banks=(4, 5)):
                self.done = NG * turn
                self.src, self.xn, self.xt_hi, self.xt_lo = src, xn, xt_hi, xt_lo
                self.affine, self.rms_row, self.banks = affine, rms_row, banks
                self.stats_ready = shared("ln_stats")
                self.rstd_ready = shared("ln_rstd")
                self.xn_ready = shared("ln_xn")
                self.affine_done = shared("ln_affine")
                self.tp_ready = shared("ln_tp")
                self.hi_ready = shared("ln_xthi")
                self.xt_ready = shared("ln_xt")
                self.pool_steps = shared("ln_poolsteps")
                self.rms_rstd = shared("ln_rmsrstd")
                self.sq_ready = shared("ln_sq")
                self.dve_steps = 6 if rms_row is not None else 2

            def vector_norm(self, dve, steps, g, quantise=None):
                src = [self.src[:, bass.ds(GT * g + j, 1), :] for j in range(GT)]
                for j in range(GT):
                    ins = dve.bn_stats(stats[:, j, :], src[j])
                steps(ins, hold=held)
                for j in range(GT):
                    ins = dve.bn_aggr(meanvar[:, j, :], stats[:, j, :])
                steps(ins)
                dve.tensor_scalar(vareps[:, :], meanvar[:, :, 1], EPS, None, ALU.add).then_inc(self.stats_ready, 1)
                dve.wait_ge(self.rstd_ready, self.done + g + 1)
                dve.wait_ge(self.tp_ready, KC * (self.done + g))
                for j in range(GT):
                    ins = dve.tensor_scalar(self.xn[:, j:j + 1, :], src[j], meanvar[:, j, 0:1], rstd[:, j:j + 1],
                                            ALU.subtract, ALU.mult)
                if quantise is not None:
                    quantise(ins)
                    dve.sem_inc(self.xn_ready, 1)
                    return
                if self.rms_row is None:
                    ins.then_inc(self.xn_ready, 1)
                    return
                steps(ins)
                for j in range(GT):
                    ins = dve.bn_stats(stats[:, j, :], self.xn[:, j, :])
                steps(ins, hold=held)
                for j in range(GT):
                    ins = dve.bn_aggr(meanvar[:, j, :], stats[:, j, :])
                steps(ins)
                steps(dve.tensor_tensor(rms[:, :], meanvar[:, :, 0], meanvar[:, :, 0], ALU.mult))
                dve.scalar_tensor_tensor(vareps[:, :], rms[:, :], 1e-8, meanvar[:, :, 1], ALU.add, ALU.add
                                         ).then_inc(self.sq_ready, 1)
                dve.wait_ge(self.rms_rstd, g + 1)
                for j in range(GT):
                    ins = dve.scalar_tensor_tensor(self.xn[:, j, :], self.xn[:, j, :], rstd[:, j:j + 1], self.rms_row,
                                                   ALU.mult, ALU.mult)
                ins.then_inc(self.xn_ready, 1)

            def gpsimd(self, pool, g):
                pool.wait_ge(self.stats_ready, self.done + g + 1)
                steps = Steps(pool, self.pool_steps, (1 if self.affine else 0) * g)
                pool.tensor_tensor(rstd[:, :], vareps[:, :], neghalf[:, :], ALU.pow).then_inc(self.rstd_ready, 1)
                if self.rms_row is not None:
                    pool.wait_ge(self.sq_ready, g + 1)
                    pool.tensor_tensor(rstd[:, :], vareps[:, :], neghalf[:, :], ALU.pow).then_inc(self.rms_rstd, 1)
                if self.affine:
                    gain, shift = self.affine
                    pool.wait_ge(self.xn_ready, self.done + g + 1)
                    steps(pool.tensor_tensor(self.xn, self.xn, gain.unsqueeze(1).to_broadcast([P, GT, D]), ALU.mult))
                    pool.tensor_tensor(self.xn, self.xn, shift.unsqueeze(1).to_broadcast([P, GT, D]), ALU.add
                                       ).then_inc(self.affine_done, 1)

            def tensor(self, pe, g):
                if self.affine:
                    pe.wait_ge(self.affine_done, g + 1)
                else:
                    pe.wait_ge(self.xn_ready, self.done + g + 1)
                pe.wait_ge(self.xt_ready, KC * (self.done + g))
                for k in range(KC):
                    for j in range(GT):
                        ins = pe.transpose(PS[:, self.banks[k], j * P:(j + 1) * P], self.xn[:, j, k * P:(k + 1) * P], ident[:, :])
                    ins.then_inc(self.tp_ready, 1)

            def scalar(self, act, g):
                for k in range(KC):
                    act.wait_ge(self.tp_ready, KC * (self.done + g) + k + 1)
                    act.activation(self.xt_hi(g, k), PS[:, self.banks[k], :], ACT.Copy).then_inc(self.hi_ready, 1)

            def vector_lo(self, dve, g):
                for k in range(KC):
                    dve.wait_ge(self.hi_ready, KC * (self.done + g) + k + 1)
                    dve.tensor_tensor(self.xt_lo(g, k), PS[:, self.banks[k], :], self.xt_hi(g, k).bitcast(F32),
                                      ALU.subtract).then_inc(self.xt_ready, 1)

        def split_matmuls(pe, dst, kcs, stat, mov, first=True, last=True):
            n = 0
            todo = [(k, a, b) for k in kcs for a, b in HL]
            for k, a, b in todo:
                ins = pe.matmul(dst, stat(a, k), mov(b, k), start=(first and n == 0), stop=(last and n == len(todo) - 1))
                n += 1
            return ins

        def prologue():
            raw = fview(0, 2, LAYERS, KC, D)
            ctx_raw = fview(4096, KC, NB, 2, S2)
            bv_row = fview(4608, LAYERS, D)
            wr = rview(0, 2, 2, LAYERS, KC, D)
            cx = rview(8192, 2, KC, NB * 2 * S2)
            loads = [sem(f"pro_load{i}") for i in range(14)]
            const_ready = sem("pro_const")
            gates_ready = sem("pro_gates")
            hi_ready, split_ready = sem("pro_hi"), sem("pro_split")
            kt_ready, kt_done = sem("pro_kt"), sem("pro_ktdone")
            v_ready, v_done = sem("pro_v"), sem("pro_vdone")

            def sync(sp):
                n = [0]

                def load(dst, src):
                    sp.dma_start(dst, src).then_inc(loads[n[0]], 16)
                    n[0] += 1

                load(ctx_raw[:, :, :, 0, :], A["ctxT"])
                load(ctx_raw[:, :, :, 1, :], A["ctxT"])
                load(raw[:, 0], A["Wk"])
                load(raw[:, 1], A["Wv"])
                load(bias_cols[:, 0:B1_COL], A["bqk"])
                load(bv_row, A["bv"].partition_broadcast(P))
                load(gates[:, 0:LAYERS], A["g_xattn"].partition_broadcast(P))
                load(gates[:, LAYERS:2 * LAYERS], A["g_ffn"].partition_broadcast(P))
                load(X[:, :, :], A["x"])
                load(mask[:, :, :], A["mask"])
                load(bias_cols[:, B1_COL:B1_COL + 8], A["b1"])
                load(bias_cols[:, EB_COL:EB_COL + 8], A["sb1"])
                load(bias_cols[:, EB_COL + 8:EB_COL + 72], A["eb1"])
                for s in loads[:n[0]]:
                    sp.wait_ge(s, 16)

            def gpsimd(pool):
                pool.memset(ident[:, :], 0.0)
                pool.memset(headmask[:, :], 1.0)
                pool.memset(neghalf[:, :], -0.5)
                pool.memset(negbig[:, :], -1e18)
                pool.memset(router_r[:, :, :, :].bitcast(F32), 0.0)
                steps = Steps(pool, const_ready)
                steps(pool.memset(VBF[:, :], 0.0))
                steps(pool.affine_select(out=ident[:, :], in_=ident[:, :], pattern=[[-1, P]], compare_op=ALU.not_equal,
                                         fill=1.0, base=0, channel_multiplier=1))
                steps(pool.affine_select(out=headmask[:, :], in_=headmask[:, :], pattern=[[-DK, HC]],
                                         compare_op=ALU.is_ge, fill=0.0, base=0, channel_multiplier=1))
                steps(pool.affine_select(out=headmask[:, :], in_=headmask[:, :], pattern=[[DK, HC]],
                                         compare_op=ALU.is_ge, fill=0.0, base=DK - 1, channel_multiplier=-1))
                steps(pool.iota(iota8[:, :], [[1, NE]], base=0, channel_multiplier=0,
                                allow_small_or_imprecise_dtypes=True))
                for c in range(H // 2):
                    for half in range(2):
                        at = P + 2 * (c % 4) + half
                        steps(pool.memset(VB[half * S2:(half + 1) * S2, :, c, at:at + 1], 1.0))

            def scalar(act):
                act.wait_ge(loads[6], 16)
                act.wait_ge(loads[7], 16)
                act.activation(gates[:, :], gates[:, :], ACT.Tanh).then_inc(gates_ready, 1)
                for i in range(2):
                    act.wait_ge(loads[i], 16)
                act.activation(cx[:, 0], ctx_raw.rearrange("p k b t s -> p k (b t s)"), ACT.Copy).then_inc(hi_ready, 1)
                for i in range(2):
                    act.wait_ge(loads[2 + i], 16)
                    act.activation(wr[:, 0, i], raw[:, i], ACT.Copy).then_inc(hi_ready, 1)
                act.wait_ge(loads[4], 16)
                for l in range(LAYERS):
                    for oc in range(KC):
                        act.wait_ge(kt_ready, KC * l + oc + 1)
                        col = bk_col(l) + oc
                        act.activation(KT[:, l, oc, :], PS[:, oc, 0:P], ACT.Identity,
                                       bias=bias_cols[:, col:col + 1]).then_inc(kt_done, 1)

            def vector(dve):
                dve.wait_ge(hi_ready, 1)
                dve.tensor_tensor(cx[:, 1], ctx_raw.rearrange("p k b t s -> p k (b t s)"), cx[:, 0].bitcast(F32),
                                  ALU.subtract).then_inc(split_ready, 1)
                for i in range(2):
                    dve.wait_ge(hi_ready, 2 + i)
                    dve.tensor_tensor(wr[:, 1, i], raw[:, i], wr[:, 0, i].bitcast(F32), ALU.subtract).then_inc(split_ready, 1)
                dve.wait_ge(loads[5], 16)
                for l in range(LAYERS):
                    for b in range(NB):
                        dve.wait_ge(v_ready, NB * l + b + 1)
                        dve.tensor_tensor(VD[:, l, b, :], PS[:, 2 + b, 0:D], bv_row[:, l, :], ALU.add).then_inc(v_done, 1)

            def tensor(pe):
                pe.wait_ge(split_ready, 3)
                for l in range(LAYERS):
                    for oc in range(KC):
                        pe.wait_ge(kt_done, max(KC * (l - 1) + oc + 1, 0))
                        split_matmuls(pe, PS[:, oc, 0:P], range(KC),
                                      lambda a, k: wr[:, a, 0, l, k, oc * P:(oc + 1) * P],
                                      lambda b, k: cx[:, b, k, :].rearrange("p (b t s) -> p b t s", b=NB, t=2)[:, :, 0, :],
                                      ).then_inc(kt_ready, 1)
                    for b in range(NB):
                        pe.wait_ge(v_done, max(NB * (l - 1) + b + 1, 0))
                        split_matmuls(pe, PS[:, 2 + b, 0:D], range(KC),
                                      lambda a, k: cx[:, a, k, b * P:(b + 1) * P],
                                      lambda m, k: wr[:, m, 1, l, k, :]).then_inc(v_ready, 1)

            return dict(sync=sync, gpsimd=gpsimd, scalar=scalar, vector=vector, tensor=tensor)

        def attention(l):
            n_ = "at_"
            first = l == 0
            masked = l == 3
            xt = rview(0, 2, KC, GW)
            qt = rview(2048, 2, KC, GW)
            kb = rview(4096, NB, 2, KC, SC)
            wq = rview(8192, 2, KC, D)
            wo = rview(9216, 2, KC, D)
            ot = rview(10240, 2, KC, P)
            probs = fview(0, 2, H * S2)
            pt = fview(2048, H // 2, P)
            xn = fview(3072, GT, D)
            q32 = fview(4096, KC, GW)
            bias_in = fview(5120, 2, H * S2)
            raw = fview(7168, 2, KC, D)
            osb = fview(8192, 2, D)
            bo_row = fview(8704, D)
            tmp = fview(8960, D)
            mx = [small[:, p * H:(p + 1) * H] for p in range(2)]
            rsum = small[:, 32:32 + H]
            bq4 = small[:, 48:48 + KC]

            w_in = [shared(n_ + f"w_in{i}") for i in range(3)]
            w_hi, w_ready, bq_ready = shared(n_ + "w_hi"), shared(n_ + "w_ready"), shared(n_ + "bq")
            kb_ready, kb_lo_ready, vb_ready = shared(n_ + "kb_hi"), shared(n_ + "kb"), shared(n_ + "vb")
            steps_sem = shared(n_ + "steps")
            q_ready, q32_ready, q_split = shared(n_ + "q"), shared(n_ + "q32"), shared(n_ + "qsplit")
            s_ready, sub_done, p_ready = shared(n_ + "s"), shared(n_ + "sub"), shared(n_ + "p")
            pt_ready, pt_sb = shared(n_ + "pt"), shared(n_ + "ptsb")
            o_ready, o_norm = shared(n_ + "o"), shared(n_ + "onorm")
            ot_ready, ot_hi, ot_split = shared(n_ + "ot"), shared(n_ + "othi"), shared(n_ + "otsplit")
            y_ready, fin_done = shared(n_ + "y"), shared(n_ + "fin")
            bias_here = [shared(n_ + f"bias{i}") for i in range(2)]
            bias_free = shared(n_ + "biasfree")
            norm = Norm(TURNS[f"at{l}"], X, xn, lambda g, k: xt[:, 0, k, :], lambda g, k: xt[:, 1, k, :])

            def sync(sp):
                sp.dma_start(raw[:, 0], A[f"Wq{l}"]).then_inc(w_in[0], 16)
                sp.dma_start(raw[:, 1], A[f"Wo{l}"]).then_inc(w_in[1], 16)
                if not first:
                    sp.dma_start(bo_row, A[f"bo{l}"].partition_broadcast(P)).then_inc(w_in[2], 16)
                else:
                    with sp.Fori(0, NG) as g:
                        for j in range(GT):
                            sp.wait_ge(bias_free, GT * g + j + 1)
                            sp.dma_start(bias_in[:, j % 2, :].unsqueeze(1), A["fside"][:, bass.ds(GT * g + j, 1), :]
                                         ).then_inc(bias_here[j % 2], 16)

            def gpsimd(pool):
                with pool.Fori(0, NG) as g:
                    norm.gpsimd(pool, g)

            def scalar(act):
                for i in range(2):
                    act.wait_ge(w_in[i], 16 * (l + 1))
                    act.activation([wq, wo][i][:, 0], raw[:, i], ACT.Copy).then_inc(w_hi, 1)
                act.activation(bq4, bias_cols[:, bq_col(l):bq_col(l) + KC], ACT.Copy, scale=SCALE).then_inc(bq_ready, 1)
                act.wait_ge(bq_ready, l + 1)
                with act.Fori(0, NG) as g:
                    G = NG * l + g
                    norm.scalar(act, g)
                    for oc in range(KC):
                        act.wait_ge(q_ready, KC * G + oc + 1)
                        act.activation(q32[:, oc, :], PS[:, 6 + oc, :], ACT.Identity, bias=bq4[:, oc:oc + 1],
                                       scale=SCALE).then_inc(q32_ready, 1)

                    def exp(j):
                        act.wait_ge(sub_done, GT * G + j + 1)
                        act.activation(probs[:, j % 2, :], probs[:, j % 2, :], ACT.Exp).then_inc(p_ready, 1)

                    def ot_hi_copy(j):
                        act.wait_ge(ot_ready, GT * G + j + 1)
                        act.activation(ot[:, 0], PS[:, 7, 0:D].rearrange("p (k t) -> p k t", k=KC), ACT.Copy).then_inc(ot_hi, 1)

                    exp(0)
                    for j in range(GT):
                        act.wait_ge(pt_ready, GT * G + j + 1)
                        act.activation(pt, PS[:, 4:6, :].rearrange("p b (c t) -> p (b c) t", t=P), ACT.Copy).then_inc(pt_sb, 1)
                        if j + 1 < GT:
                            exp(j + 1)
                        if j:
                            ot_hi_copy(j - 1)
                    ot_hi_copy(GT - 1)

            soft_steps = 1 + (1 if first else 0) + (1 if masked else 0)
            per_group = norm.dve_steps + KC + GT * (soft_steps + 1 + (0 if first else 1))
            steps_before = sum(steps_done)
            steps_done.append(NG * per_group)

            def vector(dve):
                for i in range(2):
                    dve.wait_ge(w_hi, 2 * l + i + 1)
                    w = [wq, wo][i]
                    dve.tensor_tensor(w[:, 1], raw[:, i], w[:, 0].bitcast(F32), ALU.subtract).then_inc(w_ready, 1)
                for b in range(NB):
                    for k in range(KC):
                        for h in range(HC):
                            ins = dve.tensor_scalar(kb[:, b, 0, k, h * S2:(h + 1) * S2], KT[:, l, k, b * S2:(b + 1) * S2],
                                                    headmask[:, h:h + 1], None, ALU.mult)
                ins.then_inc(kb_ready, 1)
                dve.wait_ge(kb_ready, l + 1)
                for b in range(NB):
                    for k in range(KC):
                        for h in range(HC):
                            ins = dve.scalar_tensor_tensor(kb[:, b, 1, k, h * S2:(h + 1) * S2], KT[:, l, k, b * S2:(b + 1) * S2],
                                                           headmask[:, h:h + 1], kb[:, b, 0, k, h * S2:(h + 1) * S2].bitcast(F32),
                                                           ALU.mult, ALU.subtract)
                ins.then_inc(kb_lo_ready, 1)
                wide = VC + 2 * DK
                for half in range(2):
                    rows = slice(half * S2, (half + 1) * S2)
                    for b in range(NB):
                        vd = VD[rows, l, b, :].rearrange("p (c t d) -> p t c d", t=2, d=DK)[:, half]
                        for k in range(KC):
                            at = (b * H // 2 + k * 4) * VC + half * DK
                            ins = dve.tensor_copy(VBF[rows, at:at + 4 * wide].rearrange("p (c w) -> p c w", w=wide)[:, :, 0:DK],
                                                  vd[:, 4 * k:4 * k + 4, :])
                ins.then_inc(vb_ready, 1)
                if first:
                    dve.sem_inc(bias_free, 2)
                else:
                    dve.wait_ge(w_in[2], 16 * l)
                with dve.Fori(0, NG) as g:
                    G = NG * l + g
                    steps = Steps(dve, steps_sem, steps_before + per_group * g)
                    if masked:
                        dve.tensor_copy(mask_g[:, :, :], mask[:, bass.ds(GT * g, GT), :])
                    norm.vector_norm(dve, steps, g)
                    norm.vector_lo(dve, g)
                    for oc in range(KC):
                        dve.wait_ge(q32_ready, KC * G + oc + 1)
                        steps(dve.tensor_copy(qt[:, 0, oc, :], q32[:, oc, :]))
                        dve.tensor_tensor(qt[:, 1, oc, :], q32[:, oc, :], qt[:, 0, oc, :].bitcast(F32), ALU.subtract).then_inc(q_split, 1)

                    def softmax_shift(j):
                        sc = PS[:, 2 * (j % 2):2 * (j % 2) + 2, :].rearrange("p k (h s) -> p (k h) s", s=S2)
                        pr = probs[:, j % 2, :].rearrange("p (h s) -> p h s", s=S2)
                        dve.wait_ge(s_ready, GT * G + j + 1)
                        if first:
                            dve.wait_ge(bias_here[j % 2], 16 * (GT // 2 * g + j // 2 + 1))
                            steps(dve.tensor_tensor(pr, sc, bias_in[:, j % 2, :].rearrange("p (h s) -> p h s", s=S2), ALU.add))
                            dve.sem_inc(bias_free, 1)
                            sc = pr
                        if masked:
                            m = mask_g[:, j:j + 1, :].to_broadcast([P, H, S2])
                            dve.sem_inc(held, 1)
                            steps(dve.copy_predicated(sc, m, negbig[:, 0:1].unsqueeze(2).to_broadcast([P, H, S2])))
                        steps(dve.tensor_reduce(mx[j % 2], sc, AX, ALU.max))
                        dve.tensor_tensor(pr, sc, mx[j % 2].unsqueeze(2).to_broadcast([P, H, S2]), ALU.subtract).then_inc(sub_done, 1)

                    def normalise(j):
                        dve.wait_ge(o_ready, GT * G + j + 1)
                        o = PS[:, 6, 0:KC * VC].rearrange("p (k v) -> p k v", k=KC)
                        steps(dve.reciprocal(rsum.rearrange("p (k h) -> p k h", k=KC), o[:, :, P:VC]))
                        for k in range(KC):
                            ins = dve.tensor_tensor(osb[:, j % 2, k * P:(k + 1) * P].rearrange("p (h d) -> p h d", h=HC),
                                                    o[:, k, 0:P].rearrange("p (h d) -> p h d", h=HC),
                                                    rsum[:, k * HC:(k + 1) * HC].unsqueeze(2).to_broadcast([P, HC, DK]), ALU.mult)
                        ins.then_inc(o_norm, 1)

                    def finish(j):
                        dve.wait_ge(ot_hi, GT * G + j + 1)
                        dve.tensor_tensor(ot[:, 1], PS[:, 7, 0:D].rearrange("p (k t) -> p k t", k=KC), ot[:, 0].bitcast(F32),
                                          ALU.subtract).then_inc(ot_split, 1)
                        dve.wait_ge(y_ready, GT * G + j + 1)
                        if first:
                            dve.tensor_tensor(Y[:, bass.ds(GT * g + j, 1), :], PS[:, 7, D:2 * D].unsqueeze(1), xn[:, j:j + 1, :],
                                              ALU.add).then_inc(fin_done, 1)
                        else:
                            steps(dve.tensor_tensor(tmp, PS[:, 7, D:2 * D], bo_row, ALU.add))
                            x = X[:, bass.ds(GT * g + j, 1), :]
                            dve.scalar_tensor_tensor(x, tmp.unsqueeze(1), gates[:, l:l + 1], x, ALU.mult, ALU.add).then_inc(fin_done, 1)

                    softmax_shift(0)
                    for j in range(GT):
                        if j + 1 < GT:
                            softmax_shift(j + 1)
                        normalise(j)
                        if j:
                            finish(j - 1)
                    finish(GT - 1)
                    assert steps.n == per_group, (steps.n, per_group)

            def tensor(pe):
                pe.wait_ge(w_ready, 2 * (l + 1))
                pe.wait_ge(kb_lo_ready, l + 1)
                pe.wait_ge(vb_ready, l + 1)
                with pe.Fori(0, NG) as g:
                    G = NG * l + g
                    b = g // 2
                    norm.tensor(pe, g)
                    pe.wait_ge(norm.xt_ready, KC * (norm.done + g + 1))
                    pe.wait_ge(fin_done, GT * G)
                    for oc in range(KC):
                        split_matmuls(pe, PS[:, 6 + oc, :], range(KC), lambda a, k: wq[:, a, k, oc * P:(oc + 1) * P],
                                      lambda m, k: xt[:, m, k, :]).then_inc(q_ready, 1)

                    def scores(j):
                        for k in range(KC):
                            ins = split_matmuls(pe, PS[:, 2 * (j % 2) + k, :], [k], lambda a, k: qt[:, a, k, j * P:(j + 1) * P],
                                                lambda m, k: kb[:, bass.ds(b, 1), m, k, :])
                        ins.then_inc(s_ready, 1)

                    def project(j):
                        pe.wait_ge(o_norm, GT * G + j + 1)
                        pe.wait_ge(fin_done, GT * G + j)
                        for k in range(KC):
                            ins = pe.transpose(PS[:, 7, k * P:(k + 1) * P], osb[:, j % 2, k * P:(k + 1) * P], ident[:, :])
                        ins.then_inc(ot_ready, 1)
                        pe.wait_ge(ot_split, GT * G + j + 1)
                        split_matmuls(pe, PS[:, 7, D:2 * D], range(KC), lambda a, k: ot[:, a, k, :],
                                      lambda m, k: wo[:, m, k, :]).then_inc(y_ready, 1)

                    pe.wait_ge(q_split, KC * (G + 1))
                    scores(0)
                    for j in range(GT):
                        if j + 1 < GT:
                            scores(j + 1)
                        pe.wait_ge(p_ready, GT * G + j + 1)
                        for c in range(H // 2):
                            ins = pe.transpose(PS[:, 4 + c // 4, (c % 4) * P:(c % 4 + 1) * P], probs[:, j % 2, c * P:(c + 1) * P],
                                               ident[:, :])
                        ins.then_inc(pt_ready, 1)
                        pe.wait_ge(pt_sb, GT * G + j + 1)
                        pe.wait_ge(o_norm, GT * G + j)
                        for k in range(KC):
                            for c in range(4):
                                ins = pe.matmul(PS[:, 6, k * VC:(k + 1) * VC].unsqueeze(1), pt[:, 4 * k + c, :],
                                                VB[:, bass.ds(b, 1), 4 * k + c, :], start=(c == 0), stop=(c == 3))
                        ins.then_inc(o_ready, 1)
                        if j:
                            project(j - 1)
                    project(GT - 1)

            return dict(sync=sync, gpsimd=gpsimd, scalar=scalar, vector=vector, tensor=tensor)

        phases += [prologue(), attention(0)]

        XT = rview(0, 2, KC, TOK)

        def wait_all(eng, sems):
            for s in sems:
                eng.wait_ge(s, 16)

        class Router:

            def __init__(self, l, kind, biases):
                self.turn = {"softmax": 0, "top": 1, "sigmoid": 2}[kind]
                self.bias_turn = {"softmax": 1, "top": 0, "sigmoid": 2}[kind]
                self.l, self.kind, self.biases = l, kind, biases
                self.lt = fview(7168, TOK)
                self.w_raw = small[:, 0:KC * NE].rearrange("p (k e) -> p k e", k=KC)
                self.br = small[:, 16:17]
                self.rows = fview(6912, D)
                self.p = Y[:, 0, 0:NT * NE].rearrange("p (t e) -> p t e", t=NT)
                self.e = Y[:, 1, 0:NT * NE].rearrange("p (t e) -> p t e", t=NT)
                self.vals = Y[:, 2, 0:NT * NE].rearrange("p (t e) -> p t e", t=NT)
                self.idx = Y[:, 3, 0:NT * NE].bitcast(U32).rearrange("p (t e) -> p t e", t=NT)
                self.idxf = Y[:, 4, 0:NT * 2].rearrange("p (t e) -> p t e", t=NT)
                self.sel = Y[:, 5, 0:NT * NE].rearrange("p (t e) -> p t e", t=NT)
                self.one = Y[:, 6, 0:NT * NE].rearrange("p (t e) -> p t e", t=NT)
                self.r = Y[:, 7, 0:2 * NT].rearrange("p (i t) -> p i t", i=2)
                self.cw = Y[:, 8, 0:NT * (NE + 1)].rearrange("p (t e) -> p t e", t=NT)
                self.w_in = [shared(f"router_in{i}") for i in range(4)]
                (self.w_hi, self.w_ready, self.lg, self.s_lt, self.tok, self.sub, self.exp, self.cw_ready, self.ct, self.ctsb,
                 self.add, self.added) = (shared("router_" + n) for n in (
                     "w_hi", "w_ready", "lg", "lt", "tok", "sub", "exp", "cw", "ct", "ctsb", "add", "added"))
                self.steps = sem(f"router_steps_{kind}")

            def sync(self, sp):
                l = self.l
                sp.dma_start(self.w_raw, A[f"router{l}"]).then_inc(self.w_in[0], 16)
                if l == 0:
                    sp.dma_start(self.br[0:NE, :], A["router_b"]).then_inc(self.w_in[1], 16)
                if self.biases:
                    sp.dma_start(self.rows[0:self.biases, :], A[f"bias_rows{l}"]).then_inc(self.w_in[2], 16)

            def scalar_weights(self, act):
                act.wait_ge(self.w_in[0], 16 * (self.turn + 1))
                act.activation(router_r[:, 0, :, 0:NE], self.w_raw, ACT.Copy).then_inc(self.w_hi, 1)

            def vector_weights(self, dve):
                dve.wait_ge(self.w_hi, self.turn + 1)
                dve.tensor_tensor(router_r[:, 1, :, 0:NE], self.w_raw, router_r[:, 0, :, 0:NE].bitcast(F32),
                                  ALU.subtract).then_inc(self.w_ready, 1)

            def tensor(self, pe):
                pe.wait_ge(self.w_ready, self.turn + 1)
                for g in range(NG):
                    ins = split_matmuls(pe, PS[:, g, :], range(KC), lambda a, k: router_r[:, a, k, :],
                                        lambda m, k: XT[:, m, k, g * GW:(g + 1) * GW])
                ins.then_inc(self.lg, 1)
                pe.wait_ge(self.s_lt, self.turn + 1)
                for t in range(NT):
                    ins = pe.transpose(PS[:, 4, t * NE:(t + 1) * NE], self.lt[0:NE, t * P:(t + 1) * P], ident[0:NE, 0:NE])
                ins.then_inc(self.tok, 1)
                if self.biases:
                    n = self.biases
                    pe.wait_ge(self.cw_ready, self.bias_turn)
                    for t in range(NT):
                        ins = pe.transpose(PS[0:n, t // 4, (t % 4) * P:(t % 4 + 1) * P], self.cw[:, t, 0:n], ident[:, :])
                    ins.then_inc(self.ct, 1)
                    pe.wait_ge(self.ctsb, self.bias_turn)
                    for t in range(NT):
                        ins = pe.matmul(PS[:, t // 2, (t % 2) * D:(t % 2 + 1) * D], self.lt[0:n, t * P:(t + 1) * P],
                                        self.rows[0:n, :], start=(t % 2 == 0), stop=True, skip_group_check=True)
                    ins.then_inc(self.add, 1)

            def scalar(self, act):
                act.wait_ge(self.lg, self.turn + 1)
                lg = PS[0:NE, 0:4, :].rearrange("p b n -> p (b n)")
                if self.l == 0:
                    act.wait_ge(self.w_in[1], 16)
                    act.activation(self.lt[0:NE, :], lg, ACT.Identity, bias=self.br[0:NE, :]).then_inc(self.s_lt, 1)
                else:
                    act.activation(self.lt[0:NE, :], lg, ACT.Copy).then_inc(self.s_lt, 1)
                if self.kind == "sigmoid":
                    act.wait_ge(self.tok, self.turn + 1)
                    act.activation(self.p, PS[:, 4, 0:NT * NE].rearrange("p (t e) -> p t e", t=NT), ACT.Sigmoid).then_inc(self.exp, 1)
                else:
                    act.wait_ge(self.sub, self.turn + 1)
                    act.activation(self.e, self.e, ACT.Exp).then_inc(self.exp, 1)
                if self.biases:
                    act.wait_ge(self.ct, self.bias_turn)
                    act.wait_ge(self.w_in[2], 16 * self.bias_turn)
                    act.activation(self.lt[0:self.biases, :], PS[0:self.biases, 0:4, :].rearrange("p b n -> p (b n)"),
                                   ACT.Copy).then_inc(self.ctsb, 1)

            def vector(self, dve):
                steps = Steps(dve, self.steps)
                full = [P, NT, NE]
                lg = PS[:, 4, 0:NT * NE].rearrange("p (t e) -> p t e", t=NT)
                gate = gates[:, LAYERS + self.l:LAYERS + self.l + 1]
                if self.kind != "sigmoid":
                    dve.wait_ge(self.tok, self.turn + 1)
                    m = self.r[:, 0, :]
                    steps(dve.tensor_reduce(m, lg, AX, ALU.max))
                    dve.tensor_tensor(self.e, lg, m.unsqueeze(2).to_broadcast(full), ALU.subtract).then_inc(self.sub, 1)
                    dve.wait_ge(self.exp, self.turn + 1)
                    steps(dve.tensor_reduce(m, self.e, AX, ALU.add))
                    steps(dve.reciprocal(self.r[:, 1, :], m))
                    steps(dve.tensor_tensor(self.p, self.e, self.r[:, 1, :].unsqueeze(2).to_broadcast(full), ALU.mult))
                else:
                    dve.wait_ge(self.exp, self.turn + 1)
                for t in range(NT):
                    ins = dve.max(self.vals[:, t, :], self.p[:, t, :])
                steps(ins)
                for t in range(NT):
                    ins = dve.max_index(self.idx[:, t, :], self.vals[:, t, :], self.p[:, t, :])
                steps(ins)
                steps(dve.tensor_copy(self.idxf, self.idx[:, :, 0:2]))
                it = iota8[:, :].unsqueeze(1).to_broadcast(full)
                dve.tensor_tensor(self.sel, it, self.idxf[:, :, 0:1].to_broadcast(full), ALU.is_equal)
                steps(dve.tensor_tensor(self.one, it, self.idxf[:, :, 1:2].to_broadcast(full), ALU.is_equal))
                steps(dve.tensor_tensor(self.sel, self.sel, self.one, ALU.add))
                steps(dve.tensor_tensor(self.p, self.p, self.sel, ALU.mult))
                if self.kind != "softmax":
                    s = self.r[:, 0, :]
                    if self.kind == "sigmoid":
                        steps(dve.scalar_tensor_tensor(s, self.vals[:, :, 0], 1e-6, self.vals[:, :, 1], ALU.add, ALU.add))
                    else:
                        steps(dve.tensor_tensor(s, self.vals[:, :, 0], self.vals[:, :, 1], ALU.add))
                    steps(dve.reciprocal(self.r[:, 1, :], s))
                    steps(dve.tensor_tensor(self.p, self.p, self.r[:, 1, :].unsqueeze(2).to_broadcast(full), ALU.mult))
                if self.l == 3:
                    dve.tensor_copy(coef[:, :, 0:2], gate.unsqueeze(2).to_broadcast([P, NT, 2]))
                    for i in range(2):
                        dst = coef[:, :, 2:2 + 2 * NE].rearrange("p t (e i) -> p t i e", i=2)[:, :, i, :]
                        ins = dve.tensor_scalar(dst, self.p, gate, None, ALU.mult)
                    steps(ins)
                else:
                    steps(dve.tensor_scalar(coef[:, :, 0:NE], self.p, gate, None, ALU.mult))
                if self.biases:
                    if self.biases > NE:
                        dve.tensor_copy(self.cw[:, :, NE:NE + 1], gate.unsqueeze(2).to_broadcast([P, NT, 1]))
                    dve.tensor_scalar(self.cw[:, :, 0:NE], self.p, gate, None, ALU.mult).then_inc(self.cw_ready, 1)
                    dve.wait_ge(self.add, self.bias_turn)
                    for q in range(4):
                        x = X[:, 4 * q:4 * q + 4, :].rearrange("p t d -> p (t d)")
                        ins = dve.tensor_tensor(x, x, PS[:, 2 * q:2 * q + 2, :].rearrange("p b n -> p (b n)"), ALU.add)
                    ins.then_inc(self.added, 1)
                    dve.wait_ge(self.added, self.bias_turn)

        def feed_forward(l, kind):
            n_ = "ff_"
            units = {"gelu": 2, "swiglu": NE, "relu": 2 + 2 * NE}[kind]
            gated = kind == "swiglu"
            NU = 2 if gated else 1
            src = Y if kind == "gelu" else X
            dst = Y if kind == "gelu" else X
            pairs = units // 2
            up = [rview(8192 + 4096 * p, 2, NU, KC, UH) for p in range(2)]
            down = [rview(16384 + 2048 * p, 2, UC, D) for p in range(2)]
            hs = [rview(20480 + 4096 * p, 2, UC, GW) for p in range(2)]
            raw_up = fview(0, NU, KC, UH)
            raw_down = fview(2048, UC, D)
            h32 = fview(3072, UC, GW)
            xn = fview(5120, GT, D)
            row = fview(6144, 3, D)
            up_in, down_in = shared(n_ + "up_in"), shared(n_ + "down_in")
            raw_free = shared(n_ + "raw_free")
            w_hi, w_ready = shared(n_ + "w_hi"), shared(n_ + "w_ready")
            u_ready, a_done, m_done = shared(n_ + "u"), shared(n_ + "a"), shared(n_ + "m")
            h_split, y_ready, acc_done = shared(n_ + "h"), shared(n_ + "y"), shared(n_ + "acc")
            steps_sem, y_bias = shared(n_ + "steps"), shared(n_ + "ybias")
            row_in = [shared(n_ + f"row{i}") for i in range(3)]
            rows = {"gelu": ["g1", "be1", "b2"], "swiglu": [], "relu": ["norm_weight"]}[kind]
            router = None if kind == "gelu" else Router(l, "top" if gated else "sigmoid", 0 if gated else NE + 1)
            norm = Norm(TURNS[kind], src, xn, lambda g, k: XT[:, 0, k, bass.ds(g * GW, GW)],
                        lambda g, k: XT[:, 1, k, bass.ds(g * GW, GW)],
                        affine=(row[:, 0], row[:, 1]) if kind == "gelu" else None,
                        rms_row=row[:, 0] if kind == "relu" else None)
            ln_sem = sem("ff_lnsteps_" + kind)
            before = {"gelu": 0, "swiglu": 2, "relu": 2 + NE}[kind]
            first = kind == "gelu"
            col = {"gelu": B1_COL, "relu": EB_COL, "swiglu": 0}[kind]

            def sync(sp):
                for n, r in enumerate(rows):
                    sp.dma_start(row[:, n], A[r].partition_broadcast(P)).then_inc(row_in[n], 16)
                if router:
                    router.sync(sp)
                with sp.Fori(0, units) as u:
                    sp.wait_ge(raw_free, before + u + 1)
                    sp.dma_start(raw_up.rearrange("p m k n -> p (m k n)").unsqueeze(1), A[f"up{l}"][:, bass.ds(u, 1), :]).then_inc(up_in, 16)
                    sp.dma_start(raw_down.rearrange("p c n -> p (c n)").unsqueeze(1), A[f"down{l}"][:, bass.ds(u, 1), :]).then_inc(down_in, 16)

            def gpsimd(pool):
                if kind == "gelu":
                    wait_all(pool, row_in)
                with pool.Fori(0, NG) as g:
                    norm.gpsimd(pool, g)
                    if kind == "gelu":
                        y = Y[:, bass.ds(GT * g, GT), :]
                        pool.tensor_tensor(y, y, row[:, 2].unsqueeze(1).to_broadcast([P, GT, D]), ALU.add).then_inc(y_bias, 1)

            def split_hi(act, p, u, guard):
                act.wait_ge(up_in, 16 * (before + u + 1))
                if guard:
                    act.wait_ge(y_ready, NG * GT * (before + u - 1))
                act.activation(up[p][:, 0], raw_up, ACT.Copy)
                if not gated:
                    act.activation(unit_bias[:, p, :], bias_cols[:, bass.ds(col + UC * u, UC)], ACT.Copy)
                act.wait_ge(down_in, 16 * (before + u + 1))
                act.activation(down[p][:, 0], raw_down, ACT.Copy).then_inc(w_hi, 1)

            def split_lo(dve, p, u):
                dve.wait_ge(w_hi, before + u + 1)
                for m in range(NU):
                    dve.tensor_tensor(up[p][:, 1, m], raw_up[:, m], up[p][:, 0, m].bitcast(F32), ALU.subtract)
                dve.tensor_tensor(down[p][:, 1], raw_down, down[p][:, 0].bitcast(F32), ALU.subtract).then_inc(w_ready, 1)
                dve.wait_ge(w_ready, before + u + 1)
                dve.sem_inc(raw_free, 1)

            def scalar(act):
                if router:
                    router.scalar_weights(act)
                split_hi(act, 0, 0, False)
                with act.Fori(0, NG) as g:
                    norm.scalar(act, g)
                if router:
                    router.scalar(act)
                if first:
                    act.sem_inc(a_done, UC)

                def unit(p, u, more):
                    act.wait_ge(w_hi, before + u + 1)
                    for g in range(NG):
                        for c in range(UC):
                            n = NG * UC * (before + u) + UC * g + c
                            bank = 2 * (c % 2) if gated else c
                            act.wait_ge(u_ready, n + 1)
                            act.wait_ge(h_split, n + 1)
                            if gated:
                                f, kw = ACT.Silu, {}
                            else:
                                f = ACT.Gelu if kind == "gelu" else ACT.Relu
                                kw = dict(bias=unit_bias[:, p, c:c + 1])
                            act.activation(h32[:, c, :], PS[:, bank, :], f, **kw).then_inc(a_done, 1)
                        if g == 1 and more:
                            split_hi(act, 1 - p, u + 1, True)

                if pairs > 1:
                    with act.Fori(0, pairs - 1) as i:
                        unit(0, 2 * i, True)
                        unit(1, 2 * i + 1, True)
                unit(0, units - 2, True)
                unit(1, units - 1, False)

            def vector(dve):
                if first:
                    dve.sem_inc(raw_free, 1)
                for s in row_in[:len(rows)]:
                    dve.wait_ge(s, 16 if first else 32)
                if router:
                    router.vector_weights(dve)
                with dve.Fori(0, NG) as g:
                    steps = Steps(dve, ln_sem, norm.dve_steps * g)
                    norm.vector_norm(dve, steps, g)
                    norm.vector_lo(dve, g)
                    assert steps.n == norm.dve_steps
                split_lo(dve, 0, 0)
                if router:
                    router.vector(dve)
                if first:
                    dve.sem_inc(h_split, UC)
                    dve.sem_inc(acc_done, GT)
                if gated:
                    dve.sem_inc(m_done, 2)
                if kind == "gelu":
                    dve.wait_ge(y_bias, NG)
                per_unit = NG * UC * (2 if gated else 1)
                all_before = {"gelu": 0, "swiglu": 2, "relu": 2 + 2 * NE}[kind] * NG * UC

                def unit(steps, p, u, more):
                    def split_h(g):
                        for c in range(UC):
                            n = NG * UC * (before + u) + UC * g + c
                            dve.wait_ge(a_done, UC + n + 1)
                            if gated:
                                ins = dve.tensor_tensor(h32[:, c, :], h32[:, c, :], PS[:, 2 * (c % 2) + 1, :], ALU.mult)
                                steps(ins)
                                dve.sem_inc(m_done, 1)
                            steps(dve.tensor_copy(hs[g % 2][:, 0, c, :], h32[:, c, :]))
                            dve.tensor_tensor(hs[g % 2][:, 1, c, :], h32[:, c, :], hs[g % 2][:, 0, c, :].bitcast(F32),
                                              ALU.subtract).then_inc(h_split, 1)

                    def accumulate(g):
                        for j in range(GT):
                            n = NG * GT * (before + u) + GT * g + j
                            t = GT * g + j
                            dve.wait_ge(y_ready, n + 1)
                            if kind == "gelu":
                                ins = dve.tensor_tensor(dst[:, t, :], PS[:, 4 + j, 0:D], dst[:, t, :], ALU.add)
                            else:
                                ins = dve.scalar_tensor_tensor(dst[:, t, :].unsqueeze(1), PS[:, 4 + j, 0:D].unsqueeze(1), coef[:, t, bass.ds(u, 1)],
                                                               dst[:, t, :].unsqueeze(1), ALU.mult, ALU.add)
                            ins.then_inc(acc_done, 1)

                    split_h(0)
                    split_h(1)
                    accumulate(0)
                    if more:
                        split_lo(dve, 1 - p, u + 1)
                    split_h(2)
                    accumulate(1)
                    split_h(3)
                    accumulate(2)
                    accumulate(3)

                if pairs > 1:
                    with dve.Fori(0, pairs - 1) as i:
                        steps = Steps(dve, steps_sem, all_before + 2 * per_unit * i)
                        unit(steps, 0, 2 * i, True)
                        unit(steps, 1, 2 * i + 1, True)
                        assert steps.n == 2 * per_unit
                steps = Steps(dve, steps_sem, all_before + 2 * per_unit * (pairs - 1))
                unit(steps, 0, units - 2, True)
                unit(steps, 1, units - 1, False)

            def tensor(pe):
                with pe.Fori(0, NG) as g:
                    norm.tensor(pe, g)
                pe.wait_ge(norm.xt_ready, norm.done * KC + KC * NG)
                if router:
                    router.tensor(pe)
                    if router.biases:
                        pe.wait_ge(router.added, router.bias_turn)
                    else:
                        pe.wait_ge(router.sub, router.turn + 1)

                def unit(p, u):
                    def go_up(g):
                        for c in range(UC):
                            n = NG * UC * (before + u) + UC * g + c
                            bank = 2 * (c % 2) if gated else c
                            pe.wait_ge(a_done, n + 1 + (2 if gated else 0))
                            if gated:
                                pe.wait_ge(m_done, NG * UC * u + UC * g + c + 1)
                            for m in range(NU):
                                ins = split_matmuls(pe, PS[:, bank + m, :], range(KC), lambda a, k: up[p][:, a, m, k, c * P:(c + 1) * P],
                                                    lambda b, k: XT[:, b, k, g * GW:(g + 1) * GW])
                            ins.then_inc(u_ready, 1)

                    def go_down(g):
                        for j in range(GT):
                            n = NG * GT * (before + u) + GT * g + j
                            pe.wait_ge(h_split, UC + NG * UC * (before + u) + UC * (g + 1))
                            pe.wait_ge(acc_done, n + 1)
                            split_matmuls(pe, PS[:, 4 + j, 0:D], range(UC), lambda a, c: hs[g % 2][:, a, c, j * P:(j + 1) * P],
                                          lambda b, c: down[p][:, b, c, :]).then_inc(y_ready, 1)

                    pe.wait_ge(w_ready, before + u + 1)
                    go_up(0)
                    go_up(1)
                    go_down(0)
                    go_up(2)
                    go_down(1)
                    go_up(3)
                    go_down(2)
                    go_down(3)

                with pe.Fori(0, pairs) as i:
                    unit(0, 2 * i)
                    unit(1, 2 * i + 1)

            return dict(sync=sync, gpsimd=gpsimd, scalar=scalar, vector=vector, tensor=tensor)

        def close_block():
            yn = fview(0, GT, D)
            row = fview(1024, 2, D)
            row_in = [sem(f"cl_row{i}") for i in range(2)]
            stats_ready, rstd_ready, yn_ready, affine_done, steps_sem = (sem("cl_" + s) for s in ("stats", "rstd", "yn", "aff", "steps"))

            def sync(sp):
                for n, r in enumerate(("g2", "be2")):
                    sp.dma_start(row[:, n], A[r].partition_broadcast(P)).then_inc(row_in[n], 16)

            def gpsimd(pool):
                with pool.Fori(0, NG) as g:
                    pool.wait_ge(stats_ready, g + 1)
                    pool.tensor_tensor(rstd[:, :], vareps[:, :], neghalf[:, :], ALU.pow).then_inc(rstd_ready, 1)

            def vector(dve):
                wait_all(dve, row_in)
                with dve.Fori(0, NG) as g:
                    steps = Steps(dve, steps_sem, 5 * g)
                    y = [Y[:, bass.ds(GT * g + j, 1), :] for j in range(GT)]
                    for j in range(GT):
                        ins = dve.bn_stats(stats[:, j, :], y[j])
                    steps(ins, hold=held)
                    for j in range(GT):
                        ins = dve.bn_aggr(meanvar[:, j, :], stats[:, j, :])
                    steps(ins)
                    dve.tensor_scalar(vareps[:, :], meanvar[:, :, 1], EPS, None, ALU.add).then_inc(stats_ready, 1)
                    dve.wait_ge(rstd_ready, g + 1)
                    for j in range(GT):
                        ins = dve.tensor_scalar(yn[:, j:j + 1, :], y[j], meanvar[:, j, 0:1], rstd[:, j:j + 1], ALU.subtract, ALU.mult)
                    steps(ins)
                    steps(dve.tensor_tensor(yn, yn, row[:, 0].unsqueeze(1).to_broadcast([P, GT, D]), ALU.mult))
                    steps(dve.tensor_tensor(yn, yn, row[:, 1].unsqueeze(1).to_broadcast([P, GT, D]), ALU.add))
                    x = X[:, bass.ds(GT * g, GT), :]
                    dve.scalar_tensor_tensor(x, yn, gates[:, 0:1], x, ALU.mult, ALU.add)

            return dict(sync=sync, gpsimd=gpsimd, vector=vector)

        def linear_experts():
            we = rview(8192, 2, KC, NE * D)
            raw = fview(0, KC, NE * D)
            xn = fview(4096, GT, D)
            n_ = "le_"
            w_in = [sem(n_ + f"in{k}") for k in range(KC)]
            w_hi, w_ready, y_ready, acc_done, ln_sem = (sem(n_ + s) for s in ("hi", "w", "y", "acc", "ln"))
            norm = Norm(TURNS["experts0"], X, xn, lambda g, k: XT[:, 0, k, bass.ds(g * GW, GW)], lambda g, k: XT[:, 1, k, bass.ds(g * GW, GW)])
            router = Router(0, "softmax", NE)
            RING = 8

            def sync(sp):
                for k in range(KC):
                    sp.dma_start(raw[:, k], A["W_experts"][:, k]).then_inc(w_in[k], 16)
                router.sync(sp)

            def gpsimd(pool):
                with pool.Fori(0, NG) as g:
                    norm.gpsimd(pool, g)

            def scalar(act):
                router.scalar_weights(act)
                with act.Fori(0, NG) as g:
                    norm.scalar(act, g)
                for k in range(KC):
                    act.wait_ge(w_in[k], 16)
                    act.activation(we[:, 0, k], raw[:, k], ACT.Copy).then_inc(w_hi, 1)
                router.scalar(act)

            def vector(dve):
                router.vector_weights(dve)
                with dve.Fori(0, NG) as g:
                    steps = Steps(dve, ln_sem, norm.dve_steps * g)
                    norm.vector_norm(dve, steps, g)
                    norm.vector_lo(dve, g)
                router.vector(dve)
                for k in range(KC):
                    dve.wait_ge(w_hi, k + 1)
                    dve.tensor_tensor(we[:, 1, k], raw[:, k], we[:, 0, k].bitcast(F32), ALU.subtract).then_inc(w_ready, 1)
                dve.sem_inc(acc_done, RING)
                with dve.Fori(0, NE // 2) as q:
                    for t in range(NT):
                        dve.wait_ge(y_ready, NT * q + t + 1)
                        for i in range(2):
                            x = X[:, t:t + 1, :]
                            ins = dve.scalar_tensor_tensor(x, PS[:, t % RING, i * D:(i + 1) * D].unsqueeze(1), coef[:, t, bass.ds(2 * q + i, 1)],
                                                           x, ALU.mult, ALU.add)
                            if i == 0:
                                ins.then_inc(ln_sem, 1)
                                dve.wait_ge(ln_sem, NG * norm.dve_steps + NT * q + t + 1)
                        ins.then_inc(acc_done, 1)

            def tensor(pe):
                with pe.Fori(0, NG) as g:
                    norm.tensor(pe, g)
                pe.wait_ge(norm.xt_ready, norm.done * KC + KC * NG)
                router.tensor(pe)
                pe.wait_ge(router.added, router.bias_turn)
                pe.wait_ge(w_ready, KC)
                with pe.Fori(0, NE // 2) as q:
                    for t in range(NT):
                        pe.wait_ge(acc_done, NT * q + t + 1)
                        split_matmuls(pe, PS[:, t % RING, :], range(KC), lambda a, k: XT[:, a, k, t * P:(t + 1) * P],
                                      lambda b, k: we[:, b, k, bass.ds(q * 2 * D, 2 * D)]).then_inc(y_ready, 1)

            return dict(sync=sync, gpsimd=gpsimd, scalar=scalar, vector=vector, tensor=tensor)

        def fp4_feed_forward():
            n_ = "q_"
            xt = rview(0, 2, KC, GW)
            guT = rview(2048, 2, 2, KC, FI)
            dT = rview(7680, 2, FN, D)
            hT = rview(11776, 2, FN, P)
            xn = fview(0, GT, D)
            raw = [fview(1024, FN, D), fview(3072, FN, D), fview(5120, KC, FI)]
            h, act_g = fview(1024, FI), fview(1728, FI)
            ax = fview(6528, 2048)
            yf = Y[:, :, :].rearrange("p t d -> p (t d)")
            sign, level, above = (yf[:, o:o + 1024].bitcast(BF16) for o in (0, 1024, 2048))
            scale, rscale, amax = (yf[:, o:o + P] for o in (3072, 3072 + P, 3072 + 2 * P))
            w_in = [sem(n_ + f"in{i}") for i in range(3)]
            x_here, abs_ready, q_done = sem(n_ + "x"), sem(n_ + "abs"), sem(n_ + "done")
            steps_sem = sem(n_ + "steps")
            wt_ready, wt_hi, wt_lo = sem(n_ + "wt"), sem(n_ + "wthi"), sem(n_ + "wtlo")
            gu_ready, silu_done, h_done = sem(n_ + "gu"), sem(n_ + "silu"), sem(n_ + "h")
            ht_ready, ht_hi, ht_split = sem(n_ + "ht"), sem(n_ + "hthi"), sem(n_ + "htsplit")
            y_ready, acc_done = sem(n_ + "y"), sem(n_ + "acc")
            parts = [FR, FR, P]
            QSTEPS = 3 + 1 + 2 * len(FP4_MID)
            norm = Norm(TURNS["fp4"], X, xn, lambda g, k: xt[:, 0, k, :], lambda g, k: xt[:, 1, k, :])
            norm.dve_steps += 1 + QSTEPS

            def sync(sp):
                for i, name in enumerate(("fp4_gate", "fp4_up", "fp4_down")):
                    sp.dma_start(raw[i][0:parts[i]], A[name]).then_inc(w_in[i], 16)

            def quantise(dve, steps, x, p, m):
                n = x.shape[1]
                nb = n // FB
                blocks = lambda v: v.rearrange("p (b i) -> p b i", i=FB)
                of_block = lambda v: v[0:p, 0:nb].unsqueeze(2).to_broadcast([p, nb, FB])
                a, s, lv, ab = ax[0:p, 0:n], sign[0:p, 0:n], level[0:p, 0:n], above[0:p, 0:n]
                steps(dve.tensor_reduce(amax[0:p, 0:nb], blocks(x), AX, ALU.max, apply_absolute_value=True))
                steps(dve.tensor_scalar(scale[0:p, 0:nb], amax[0:p, 0:nb], 1.0 / 6.0, 1e-12, ALU.mult, ALU.max))
                steps(dve.reciprocal(rscale[0:p, 0:nb], scale[0:p, 0:nb]))
                dve.wait_ge(abs_ready, m + 1)
                steps(dve.tensor_tensor(blocks(a), blocks(a), of_block(rscale), ALU.mult))
                for i, (mid, step) in enumerate(FP4_MID):
                    ins = dve.tensor_scalar(lv if i == 0 else ab, a, mid, step, ALU.is_gt, ALU.mult)
                    steps(ins)
                    if i:
                        steps(dve.tensor_tensor(lv, lv, ab, ALU.add))
                steps(dve.tensor_tensor(lv, lv, s, ALU.mult))
                ins = dve.tensor_tensor(blocks(x), blocks(lv), of_block(scale), ALU.mult)
                ins.then_inc(q_done, 1)
                dve.wait_ge(q_done, m + 1)

            def magnitudes(act, x, p, m):
                act.wait_ge(q_done, m)
                act.activation(ax[0:p, 0:x.shape[1]], x, ACT.Abs)
                act.activation(sign[0:p, 0:x.shape[1]], x, ACT.Sign).then_inc(abs_ready, 1)

            flat = lambda i: raw[i][0:parts[i]].rearrange("p a b -> p (a b)")
            per_group = norm.dve_steps + GT * (1 + QSTEPS)

            def gpsimd(pool):
                with pool.Fori(0, NG) as g:
                    norm.gpsimd(pool, g)

            def scalar(act):
                for i in range(3):
                    act.wait_ge(w_in[i], 16)
                    magnitudes(act, flat(i), parts[i], i)
                for i in range(2):
                    act.wait_ge(wt_ready, i + 1)
                    act.activation(guT[:, 0, i].rearrange("p k (b n) -> p (k b) n", b=2), PS[:, 4 * i:4 * i + 4, 0:FI // 2], ACT.Copy).then_inc(wt_hi, 1)
                act.wait_ge(wt_ready, 3)
                act.activation(dT[0:FR, 0].rearrange("p c n -> p (c n)"), PS[0:FR, 0:4, :].rearrange("p b n -> p (b n)"), ACT.Copy).then_inc(wt_hi, 1)
                with act.Fori(0, NG) as g:
                    m = 3 + 5 * g
                    act.wait_ge(x_here, g + 1)
                    magnitudes(act, xn.rearrange("p t d -> p (t d)"), P, m)
                    norm.scalar(act, g)

                    def ht_hi_copy(j):
                        act.wait_ge(ht_ready, GT * g + j + 1)
                        act.activation(hT[0:FR, 0].rearrange("p c t -> p (c t)"), PS[0:FR, 4:6, :].rearrange("p b n -> p (b n)"), ACT.Copy).then_inc(ht_hi, 1)

                    for j in range(GT):
                        act.wait_ge(gu_ready, GT * g + j + 1)
                        act.activation(act_g.rearrange("p (b n) -> p b n", b=2), PS[:, 0:2, 0:FI // 2], ACT.Silu).then_inc(silu_done, 1)
                        act.wait_ge(h_done, GT * g + j + 1)
                        magnitudes(act, h, P, m + 1 + j)
                        ht_hi_copy(j)

            def vector(dve):
                steps = Steps(dve, steps_sem)
                for i in range(3):
                    dve.wait_ge(w_in[i], 16)
                    quantise(dve, steps, flat(i), parts[i], i)
                for i in range(2):
                    dve.wait_ge(wt_hi, i + 1)
                    dve.tensor_tensor(guT[:, 1, i].rearrange("p k (b n) -> p (k b) n", b=2), PS[:, 4 * i:4 * i + 4, 0:FI // 2],
                                      guT[:, 0, i].rearrange("p k (b n) -> p (k b) n", b=2).bitcast(F32), ALU.subtract).then_inc(wt_lo, 1)
                dve.wait_ge(wt_hi, 3)
                dve.tensor_tensor(dT[0:FR, 1].rearrange("p c n -> p (c n)"), PS[0:FR, 0:4, :].rearrange("p b n -> p (b n)"),
                                  dT[0:FR, 0].rearrange("p c n -> p (c n)").bitcast(F32), ALU.subtract).then_inc(wt_lo, 1)
                before = steps.n
                with dve.Fori(0, NG) as g:
                    steps = Steps(dve, steps_sem, before + per_group * g)
                    m = 3 + 5 * g

                    def quantise_xn(ins):
                        steps(ins)
                        dve.sem_inc(x_here, 1)
                        quantise(dve, steps, xn.rearrange("p t d -> p (t d)"), P, m)

                    norm.vector_norm(dve, steps, g, quantise_xn)
                    norm.vector_lo(dve, g)

                    def finish(j):
                        dve.wait_ge(y_ready, GT * g + j + 1)
                        x = X[:, bass.ds(GT * g + j, 1), :]
                        dve.scalar_tensor_tensor(x, PS[:, 6, 0:D].unsqueeze(1), gates[:, LAYERS + 2:LAYERS + 3], x, ALU.mult, ALU.add).then_inc(acc_done, 1)

                    for j in range(GT):
                        dve.wait_ge(silu_done, GT * g + j + 1)
                        steps(dve.tensor_tensor(h.rearrange("p (b n) -> p b n", b=2), act_g.rearrange("p (b n) -> p b n", b=2),
                                                PS[:, 2:4, 0:FI // 2], ALU.mult))
                        dve.sem_inc(h_done, 1)
                        quantise(dve, steps, h, P, m + 1 + j)
                        dve.wait_ge(ht_hi, GT * g + j + 1)
                        dve.tensor_tensor(hT[0:FR, 1].rearrange("p c t -> p (c t)"), PS[0:FR, 4:6, :].rearrange("p b n -> p (b n)"),
                                          hT[0:FR, 0].rearrange("p c t -> p (c t)").bitcast(F32), ALU.subtract).then_inc(ht_split, 1)
                        if j:
                            finish(j - 1)
                    finish(GT - 1)
                    assert steps.n == per_group, (steps.n, per_group)

            def tensor(pe):
                for i in range(2):
                    pe.wait_ge(q_done, i + 1)
                    for k in range(KC):
                        for c in range(FN):
                            ins = pe.transpose(PS[:, 4 * i + 2 * k + c // 4, (c % 4) * FR:(c % 4 + 1) * FR],
                                               raw[i][0:FR, c, k * P:(k + 1) * P], ident[0:FR, 0:FR])
                    ins.then_inc(wt_ready, 1)
                pe.wait_ge(q_done, 3)
                pe.wait_ge(wt_lo, 1)
                for c in range(FN):
                    for k in range(KC):
                        ins = pe.transpose(PS[0:FR, c // 2, ((c % 2) * 2 + k) * P:((c % 2) * 2 + k + 1) * P],
                                           raw[2][:, k, c * FR:(c + 1) * FR], ident[:, :])
                ins.then_inc(wt_ready, 1)
                pe.wait_ge(wt_lo, 3)
                with pe.Fori(0, NG) as g:
                    norm.tensor(pe, g)
                    pe.wait_ge(norm.xt_ready, KC * (norm.done + g + 1))

                    def gate_up(j):
                        pe.wait_ge(h_done, GT * g + j)
                        for i in range(2):
                            for b in range(2):
                                ins = split_matmuls(pe, PS[:, 2 * i + b, 0:FI // 2], range(KC), lambda a, k: xt[:, a, k, j * P:(j + 1) * P],
                                                    lambda m, k: guT[:, m, i, k, b * (FI // 2):(b + 1) * (FI // 2)])
                        ins.then_inc(gu_ready, 1)

                    gate_up(0)
                    for j in range(GT):
                        if j + 1 < GT:
                            gate_up(j + 1)
                        pe.wait_ge(q_done, 3 + 5 * g + 2 + j)
                        for c in range(FN):
                            ins = pe.transpose(PS[0:FR, 4 + c // 4, (c % 4) * P:(c % 4 + 1) * P], h[:, c * FR:(c + 1) * FR], ident[:, :])
                        ins.then_inc(ht_ready, 1)
                        pe.wait_ge(ht_split, GT * g + j + 1)
                        pe.wait_ge(acc_done, GT * g + j)
                        split_matmuls(pe, PS[:, 6, 0:D], range(FN), lambda a, c: hT[0:FR, a, c, :], lambda b, c: dT[0:FR, b, c, :]
                                      ).then_inc(y_ready, 1)

            return dict(sync=sync, gpsimd=gpsimd, scalar=scalar, vector=vector, tensor=tensor)

        phases += [feed_forward(0, "gelu"), close_block(), linear_experts(), attention(1), feed_forward(1, "swiglu"),
                   attention(2), fp4_feed_forward(), attention(3), feed_forward(3, "relu")]

        phases = phases[:stop]
        out_done = sem("out_done")

        def run(eng, name):
            for n, phase in enumerate(phases):
                if name in phase:
                    phase[name](eng)
                eng.drain().then_inc(bar, 1)
                eng.wait_ge(bar, ENGINES * (n + 1))

        block = ctx.enter_context(nc.Block())

        @block.sync
        def _(sp):
            run(sp, "sync")
            sp.dma_start(out, X[:, :, :]).then_inc(out_done, 16)
            sp.wait_ge(out_done, 16)

        @block.gpsimd
        def _(pool):
            run(pool, "gpsimd")

        @block.scalar
        def _(act):
            run(act, "scalar")

        @block.vector
        def _(dve):
            run(dve, "vector")

        @block.tensor
        def _(pe):
            run(pe, "tensor")


def _view(arena, off, dims):
    size = 1
    for d in dims:
        size *= d
    v = arena[:, off:off + size]
    if len(dims) == 1:
        return v
    names = [f"d{i}" for i in range(len(dims))]
    return v.rearrange(f"p ({' '.join(names)}) -> p {' '.join(names)}", **dict(zip(names, dims)))


def kernel(**inputs):
    import numpy as np
    import concourse.bacc as bacc
    from concourse.bass_utils import run_bass_kernel_spmd

    nc = bacc.Bacc("TRN2", target_bir_lowering=False, num_devices=1)
    arrays = _layout(np, inputs)
    A = {name: nc.dram_tensor(f"in_{name}", a.shape, mybir.dt.from_np(a.dtype), kind="ExternalInput").ap()
         for name, a in arrays.items()}
    out = nc.dram_tensor("out_x", (P, NT, D), F32, kind="ExternalOutput").ap()
    build(nc, A, out)
    r = run_bass_kernel_spmd(nc, [{f"in_{name}": a for name, a in arrays.items()}], core_ids=[0])
    return np.ascontiguousarray(r.results[0]["out_x"].transpose(1, 0, 2)).reshape(NB, TOK // NB, D)


def _layout(np, inputs):
    i = {name: np.asarray(a) for name, a in inputs.items()}

    def rows(w, p=P):
        return np.ascontiguousarray(w.reshape(w.shape[0] // p, p, -1).transpose(1, 0, 2))

    def cols(v):
        return np.ascontiguousarray(v.reshape(-1, P).T)

    at = "L{}_xattn_{}"
    A = {"x": rows(i["x"].reshape(TOK, D)), "g_xattn": i["g_xattn"], "g_ffn": i["g_ffn"]}
    A["ctxT"] = rows(np.ascontiguousarray(i["ctx_1024"].reshape(NB * S2, D).T)).reshape(P, KC, NB, S2)
    A["fside"] = np.ascontiguousarray(i["fside_Bx16xSxS2_0"].reshape(NB, H, NT // NB, P, S2).transpose(3, 0, 2, 1, 4)
                                      ).reshape(P, NT, H * S2)
    A["mask"] = rows(i["mask_BxSxS2_bf0"].reshape(TOK, S2))
    w = {(l, n): i[at.format(l, n)].T if l == 0 else i[at.format(l, n)] for l in range(LAYERS) for n in ("Wq", "Wk", "Wv", "Wo")}
    for n in ("Wk", "Wv"):
        A[n] = np.ascontiguousarray(np.stack([rows(w[l, n]) for l in range(LAYERS)], 1))
    zero = np.zeros(D, np.float32)
    A["bqk"] = np.ascontiguousarray(np.concatenate([cols(zero if l == 0 else i[at.format(l, n)])
                                                    for l in range(LAYERS) for n in ("bq", "bk")], 1))
    A["bv"] = np.stack([zero if l == 0 else i[at.format(l, "bv")] for l in range(LAYERS)])
    for l in range(LAYERS):
        A[f"Wq{l}"], A[f"Wo{l}"] = rows(w[l, "Wq"]), rows(w[l, "Wo"])
        if l:
            A[f"bo{l}"] = i[at.format(l, "bo")]
    A["b1"], A["sb1"], A["eb1"] = cols(i["L0_xattn_b1"]), cols(i["L3_ffn_sb1"]), cols(i["L3_ffn_eb1"].reshape(-1))
    A["router0"], A["router_b"] = rows(i["L0_ffn_W_router"].T), i["L0_ffn_b_router"].reshape(NE, 1)
    A["router1"], A["router3"] = rows(i["L1_ffn_router_w"].T), rows(i["L3_ffn_router_w"].T)
    A["bias_rows0"] = i["L0_ffn_b_experts"]
    A["bias_rows3"] = np.concatenate([i["L3_ffn_eb2"], i["L3_ffn_sb2"][None]])
    A["W_experts"] = rows(i["L0_ffn_W_experts"].transpose(2, 0, 1).reshape(D, NE * D))
    for n in ("g1", "be1", "b2", "g2", "be2"):
        A[n] = i["L0_xattn_" + n]
    A["norm_weight"] = i["L3_ffn_norm_weight"]

    A["fp4_gate"], A["fp4_up"] = rows(i["L2_ffn_w_gate"], FR), rows(i["L2_ffn_w_up"], FR)
    A["fp4_down"] = rows(i["L2_ffn_w_down"])

    def units(w, axis):
        return [rows(u) for u in np.split(w, w.shape[axis] // UH, axis)]

    def stack(us):
        return np.ascontiguousarray(np.stack([u.reshape(P, -1) for u in us], 1))

    A["up0"] = stack(units(i["L0_xattn_W1"].T, 1))
    A["down0"] = stack(units(i["L0_xattn_W2"].T, 0))
    A["up1"] = stack([np.stack([rows(i["L1_ffn_gate_w"][e]), rows(i["L1_ffn_up_w"][e])], 1) for e in range(NE)])
    A["down1"] = stack([rows(i["L1_ffn_down_w"][e]) for e in range(NE)])
    A["up3"] = stack(units(i["L3_ffn_sw1"], 1) + [u for e in range(NE) for u in units(i["L3_ffn_ew1"][e], 1)])
    A["down3"] = stack(units(i["L3_ffn_sw2"], 0) + [u for e in range(NE) for u in units(i["L3_ffn_ew2"][e], 0)])
    return A
```
